# Optimizing a Trainium2 kernel written in Bass

```python
import numpy as np
import jax
import jax.numpy as jnp

def _softmax(x, axis=-1):
    return jax.nn.softmax(x, axis=axis)

def _gelu(x):
    return jax.nn.gelu(x, approximate=True)

def _silu(x):
    return jax.nn.silu(x)

def _sigmoid(x):
    return jax.nn.sigmoid(x)

def _layernorm(x, axis=-1, eps=1e-05):
    m = jnp.mean(x, axis=axis, keepdims=True)
    v = jnp.var(x, axis=axis, keepdims=True)
    return (x - m) / jnp.sqrt(v + eps)

def _scatter_add(tgt, idx, src, axis=0):
    return tgt.at[idx].add(src)

def _segment_sum(src, seg, n):
    return jax.ops.segment_sum(src, seg, n)
kernel_name = 'mk_prb_d1_jaxref_r4_53ed4b'

def setup_inputs(seed: int=0):
    np.random.seed(seed)
    _w = jnp.asarray

    def _L0_attn_setup():
        import jax, jax.numpy as jnp
        import numpy as np
        W_SEG = 512
        R = 4
        OFFSET = 0
        H = 16
        C = 256
        M = W_SEG // R

        def _mha(xi, w_in, b_in, w_out, b_out):
            b, s, m, c = xi.shape
            dh = c // H
            qkv = jnp.einsum('bsmc,ec->bsme', xi, w_in) + b_in
            q, k, v = jnp.split(qkv, 3, axis=-1)
            q = q.reshape(b, s, m, H, dh)
            k = k.reshape(b, s, m, H, dh)
            v = v.reshape(b, s, m, H, dh)
            scores = jnp.einsum('bsqhd,bskhd->bshqk', q, k) / jnp.sqrt(jnp.asarray(dh, xi.dtype))
            causal = jnp.tril(jnp.ones((m, m), dtype=bool))
            scores = jnp.where(causal, scores, jnp.asarray(-1000000000.0, xi.dtype))
            p = jax.nn.softmax(scores, axis=-1)
            o = jnp.einsum('bshqk,bskhd->bsqhd', p, v).reshape(b, s, m, c)
            return jnp.einsum('bsmc,oc->bsmo', o, w_out) + b_out
        key = jax.random.key(seed)
        k1, k2, k3, k4, k5 = jax.random.split(key, 5)
        x = jax.random.normal(k1, (4, 2048, C), dtype=jnp.float32)
        w_in = jax.random.normal(k2, (3 * C, C), dtype=jnp.float32) * C ** (-0.5)
        b_in = jnp.zeros((3 * C,), dtype=jnp.float32)
        w_out = jax.random.normal(k3, (C, C), dtype=jnp.float32) * C ** (-0.5)
        b_out = jnp.zeros((C,), dtype=jnp.float32)
        return {'x': x, 'w_in': w_in, 'b_in': b_in, 'w_out': w_out, 'b_out': b_out}
    _L0_attn_in = _L0_attn_setup()

    def _L0_ffn_setup():
        import jax, jax.numpy as jnp
        import numpy as np
        B, K, D = (128, 32, 256)
        E = 32
        H = int(D * 0.25)

        def _rsqrt_uniform(key, shape, d):
            bound = d ** (-0.5)
            return jax.random.uniform(key, shape, jnp.float32, -bound, bound)
        key = jax.random.key(seed)
        ks = jax.random.split(key, 7)
        return {'x': jax.random.normal(ks[0], (B, K, D), jnp.float32), 'router_w': _rsqrt_uniform(ks[1], (E, D), D), 'router_b': _rsqrt_uniform(ks[2], (E,), D), 'weights1': _rsqrt_uniform(ks[3], (E, D, H), H), 'bias1': _rsqrt_uniform(ks[4], (E, H), H), 'weights2': _rsqrt_uniform(ks[5], (E, H, D), D), 'bias2': _rsqrt_uniform(ks[6], (E, D), D)}
    _L0_ffn_in = _L0_ffn_setup()
    _d = {'L0_attn_x': _L0_attn_in['x'], 'L0_attn_w_in': _L0_attn_in['w_in'], 'L0_attn_b_in': _L0_attn_in['b_in'], 'L0_attn_w_out': _L0_attn_in['w_out'], 'L0_attn_b_out': _L0_attn_in['b_out'], 'L0_ffn_router_w': _L0_ffn_in['router_w'], 'L0_ffn_router_b': _L0_ffn_in['router_b'], 'L0_ffn_weights1': _L0_ffn_in['weights1'], 'L0_ffn_bias1': _L0_ffn_in['bias1'], 'L0_ffn_weights2': _L0_ffn_in['weights2'], 'L0_ffn_bias2': _L0_ffn_in['bias2']}
    _x0 = _d['L0_attn_x']
    _d['L0_attn_x'] = jax.random.normal(jax.random.fold_in(jax.random.key(seed), 1), (4, 2048, 256), dtype=_x0.dtype)
    del _x0
    return _d

def reference(L0_attn_x, L0_attn_w_in, L0_attn_b_in, L0_attn_w_out, L0_attn_b_out, L0_ffn_router_w, L0_ffn_router_b, L0_ffn_weights1, L0_ffn_bias1, L0_ffn_weights2, L0_ffn_bias2):

    def _L0_attn_ref(x, w_in, b_in, w_out, b_out):
        import jax, jax.numpy as jnp
        import numpy as np
        W_SEG = 512
        R = 4
        OFFSET = 0
        H = 16
        C = 256
        M = W_SEG // R

        def _mha(xi, w_in, b_in, w_out, b_out):
            b, s, m, c = xi.shape
            dh = c // H
            qkv = jnp.einsum('bsmc,ec->bsme', xi, w_in) + b_in
            q, k, v = jnp.split(qkv, 3, axis=-1)
            q = q.reshape(b, s, m, H, dh)
            k = k.reshape(b, s, m, H, dh)
            v = v.reshape(b, s, m, H, dh)
            scores = jnp.einsum('bsqhd,bskhd->bshqk', q, k) / jnp.sqrt(jnp.asarray(dh, xi.dtype))
            causal = jnp.tril(jnp.ones((m, m), dtype=bool))
            scores = jnp.where(causal, scores, jnp.asarray(-1000000000.0, xi.dtype))
            p = jax.nn.softmax(scores, axis=-1)
            o = jnp.einsum('bshqk,bskhd->bsqhd', p, v).reshape(b, s, m, c)
            return jnp.einsum('bsmc,oc->bsmo', o, w_out) + b_out
        b, n, c = x.shape
        s = n // W_SEG
        xr = x.reshape(b, s, W_SEG, c)
        xi = xr[:, :, OFFSET::R, :]
        oi = _mha(xi, w_in, b_in, w_out, b_out)
        out = jnp.zeros_like(xr).at[:, :, OFFSET::R, :].set(oi)
        return out.reshape(b, n, c)

    def _L0_ffn_ref(x, router_w, router_b, weights1, bias1, weights2, bias2):
        import jax, jax.numpy as jnp
        import numpy as np
        B, K, D = (128, 32, 256)
        E = 32
        H = int(D * 0.25)

        def _rsqrt_uniform(key, shape, d):
            bound = d ** (-0.5)
            return jax.random.uniform(key, shape, jnp.float32, -bound, bound)
        b, k, d = x.shape
        x_flat = x.reshape(-1, d)
        n = x_flat.shape[0]
        logits = x_flat @ router_w.T + router_b
        routed_idx = jnp.argmax(logits, axis=-1)

        def expert_mlp(w1, b1, w2, b2):
            h = jax.nn.relu(x_flat @ w1 + b1)
            return jax.nn.relu(h @ w2 + b2)
        y_all = jax.vmap(expert_mlp)(weights1, bias1, weights2, bias2)
        out_flat = y_all[routed_idx, jnp.arange(n)]
        return out_flat.reshape(b, k, d)
    x = L0_attn_x
    xn = _layernorm(x, axis=-1)
    x = x + _L0_attn_ref(xn, L0_attn_w_in, L0_attn_b_in, L0_attn_w_out, L0_attn_b_out) + _L0_ffn_ref(xn, L0_ffn_router_w, L0_ffn_router_b, L0_ffn_weights1, L0_ffn_bias1, L0_ffn_weights2, L0_ffn_bias2)
    return x

_drawn_inputs = setup_inputs


def setup_inputs(seed=0):
    import zlib

    import numpy as np

    out = dict(_drawn_inputs(seed))
    spreads = {'L0_attn_b_in': (0.0, 0.1), 'L0_attn_b_out': (0.0, 0.1)}
    factors = {'L0_ffn_bias1': 5.807}
    for name, (base, spread) in spreads.items():
        noise = np.random.default_rng([zlib.crc32(name.encode()), seed]).standard_normal(out[name].shape)
        drawn = base * np.exp(spread * noise) if base else spread * noise
        out[name] = jnp.asarray(drawn.astype(out[name].dtype))
    for name, factor in factors.items():
        out[name] = (out[name] * factor).astype(out[name].dtype)
    return out
```

```python
from contextlib import ExitStack

import concourse.bass as bass
from concourse import mybir

FP32 = mybir.dt.float32
BF16 = mybir.dt.bfloat16
I32 = mybir.dt.int32
ALU = mybir.AluOpType
ACT = mybir.ActivationFunctionType
AX = mybir.AxisListType

P = 128
D = 256
C = D // P
R = 4
NSEG = 16
NTOK = NSEG * P * R
NH = 16
DH = D // NH
E = 32
HID = D // 4
T = NTOK // P
SLOTS = 3
NPAIR = NSEG * SLOTS
NTILE = 2 * NPAIR
NIDX = NTILE + 2 * SLOTS
U1 = 4
BANKS = 4
SETUP = 23
NEG = -1e9
FAR = 1048576.0
EPS = 1e-5
assert NTILE >= T + E - 1


def head_of(j, n):
    return 8 * (n // 2) + 2 * j + n % 2


def build(nc, x, consts, w_in, b_qk, b_v, w_out, b_out, r_w, r_b, w1, b1, w2, b2, out):
    ctx = ExitStack()
    with ctx:
        def sb(name, shape, dt=FP32):
            return ctx.enter_context(nc.sbuf_tensor(name, shape, dt))

        def sem(name):
            return ctx.enter_context(nc.semaphore(name))

        ident = sb("ident", [P, P])
        identb = sb("identb", [P, P], BF16)
        causal = sb("causal", [P, P], BF16)
        before = sb("before", [P, P], BF16)
        onesb = sb("onesb", [P, P], BF16)
        zeros = sb("zeros", [P, NTILE], BF16)
        iota_i = sb("iota_i", [P, P], I32)
        iota = sb("iota", [P, P])
        part_i = sb("part_i", [P, 1], I32)
        part = sb("part", [P, 1])
        rank_i = sb("rank_i", [P, E], I32)
        rank = sb("rank", [P, E])
        tok_i = sb("tok_i", [P, T], I32)
        tok1 = sb("tok1", [P, T])
        halves = sb("halves", [P, 5])
        eps = sb("eps", [P, 4])
        power = sb("power", [P, 4])
        w_in_s = sb("w_in_s", [P, C, 3 * D])
        b_qk_s = sb("b_qk_s", [P, 2 * C])
        q_bias = sb("q_bias", [P, C])
        k_bias = sb("k_bias", [P, C, 2])
        b_v_s = sb("b_v_s", [P, D])
        w_out_s = sb("w_out_s", [P, C, D])
        b_out_s = sb("b_out_s", [P, D])
        r_w_s = sb("r_w_s", [P, C, E])
        r_b_s = sb("r_b_s", [P, E])
        w1_s = sb("w1_s", [P, C, E * HID])
        w2_s = sb("w2_s", [HID + 1, E * D])
        b1_rep = sb("b1_rep", [3 * E, HID])
        b1_hi = sb("b1_hi", [3 * E, HID], BF16)
        b1_rest = sb("b1_rest", [3 * E, HID])
        b1_mid = sb("b1_mid", [3 * E, HID], BF16)
        b1_low = sb("b1_low", [3 * E, HID])
        b1_sum = sb("b1_sum", [3 * E, HID])
        b1_part = sb("b1_part", [3 * E, HID], BF16)
        b1_s = sb("b1_s", [P, E * HID], BF16)
        xin = sb("xin", [P, U1, R, D])
        st1 = sb("st1", [P, R, 6])
        mv1 = sb("mv1", [P, U1, R, 2])
        sd1 = sb("sd1", [P, U1, R])
        rs1 = sb("rs1", [P, U1, R])
        xn1 = sb("xn1", [P, 2, R, D])
        xT1 = sb("xT1", [P, 2, C, R, P])
        xTa = sb("xTa", [P, NSEG, C, P])
        lg = sb("lg", [P, R, E])
        lmax = sb("lmax", [P, R])
        hit = sb("hit", [P, R, E])
        first = sb("first", [P, R])
        onehot = sb("onehot", [P, E, T])
        count = sb("count", [P, E, T])
        place = sb("place", [P, E, T])
        ends = sb("ends", [P, E + 1])
        rowtot = sb("rowtot", [P, E], BF16)
        cnt_i = sb("cnt_i", [P, E], I32)
        til_i = sb("til_i", [P, E], I32)
        til = sb("til", [P, E])
        cum = sb("cum", [P, E])
        offs = sb("offs", [P, E])
        base0 = sb("base0", [P, E])
        base = sb("base", [P, E])
        past = sb("past", [P, E])
        te0 = sb("te0", [P, 1])
        te1 = sb("te1", [P, 1])
        te_i = sb("te_i", [1, P], I32)
        pos = sb("pos", [P, T])
        pos_i = sb("pos_i", [P, T], I32)
        tile_i = sb("tile_i", [P, T], I32)
        slot_i = sb("slot_i", [P, T], I32)
        tile_f = sb("tile_f", [P, T])
        slot_f = sb("slot_f", [P, T])
        at_slot = sb("at_slot", [P, 2, 4, P])
        slot_col = sb("slot_col", [P, 2, 4])
        tok_at = sb("tok_at", [P, 2, 4, NTILE])
        empty = sb("empty", [P, NTILE])
        sfar = sb("sfar", [P, NTILE])
        gidx = sb("gidx", [P, NIDX], I32)
        sidx = sb("sidx", [P, NTILE], I32)
        gcol = sb("gcol", [P, SLOTS, 2], I32)
        scol = sb("scol", [P, SLOTS, 2], I32)
        xg = sb("xg", [P, SLOTS, 2, D])
        st2 = sb("st2", [P, 2, 6])
        mv2 = sb("mv2", [P, SLOTS, 2, 2])
        sd2 = sb("sd2", [P, SLOTS, 2])
        rs2 = sb("rs2", [P, SLOTS, 2])
        xn2 = sb("xn2", [P, SLOTS, 2, D])
        xT2 = sb("xT2", [P, C, 2, P])
        hid = sb("hid", [P, 2, HID])
        hT = sb("hT", [HID + 1, 2, P])
        yb = sb("yb", [P, SLOTS, 2, D])
        xa = sb("xa", [P, C, P])
        qT = sb("qT", [P, C, P])
        kT = sb("kT", [P, C, 2, P])
        v = sb("v", [P, NH, DH + 1])
        nmax = sb("nmax", [P, NH])
        rsum = sb("rsum", [P, NH])
        on = sb("on", [P, NH, DH])
        oT = sb("oT", [P, C, P])
        att = sb("att", [P, NSEG, D])
        probs = count[:, :, :].rearrange("p e t -> p (e t)").rearrange("p (n k) -> p n k", k=P)
        probsT = place[:, :, :].rearrange("p e t -> p (e t)").rearrange("p (n k) -> p n k", k=P)

        bank = [ctx.enter_context(nc.psum_tensor(f"bank{i}", [P, 512], FP32)) for i in range(8)]
        b_att, b_xT, b_h, b_y = bank[4], bank[5], bank[6], bank[7]

        x_seg = x.rearrange("b (s p r) c -> (b s) p (r c)", p=P, r=R)
        out_rows = out.rearrange("b n c -> (b n) c")
        x_rows = x.rearrange("b n c -> (b n) c")
        att_rows = out.rearrange("b (s p r) c -> p (b s) r c", p=P, r=R)[:, :, 0, :]

        passed_dve = sem("passed_dve")
        passed_pe = sem("passed_pe")
        passed_pool = sem("passed_pool")
        pool_set = sem("pool_set")
        const_in = sem("const_in")
        w_attn_in = sem("w_attn_in")
        w_rout_in = sem("w_rout_in")
        w_exp_in = sem("w_exp_in")
        b1_in = sem("b1_in")
        b1_split = sem("b1_split")
        b1_laid = sem("b1_laid")
        bias_made = sem("bias_made")
        x_in = [sem(f"x_in{u}") for u in range(U1)]
        st1_done = sem("st1_done")
        mv1_done = sem("mv1_done")
        sd1_done = sem("sd1_done")
        rs1_done = sem("rs1_done")
        xn1_done = sem("xn1_done")
        tr1_done = sem("tr1_done")
        xT1_done = sem("xT1_done")
        xTa_done = sem("xTa_done")
        lg_psum = sem("lg_psum")
        lg_done = sem("lg_done")
        rt_step = sem("rt_step")
        oh_done = sem("oh_done")
        dsp = sem("dsp")
        tot_ready = sem("tot_ready")
        tot_psum = sem("tot_psum")
        te_ready = sem("te_ready")
        te_psum = sem("te_psum")
        te_done = sem("te_done")
        pos_done = sem("pos_done")
        slot_oh = sem("slot_oh")
        slot_set = sem("slot_set")
        tok_done = sem("tok_done")
        list_mm = sem("list_mm")
        idx_done = sem("idx_done")
        gcol_set = sem("gcol_set")
        scol_set = sem("scol_set")
        gathered = [sem(f"gathered{s}") for s in range(SLOTS)]
        scattered = [sem(f"scattered{s}") for s in range(SLOTS)]
        st2_done = sem("st2_done")
        mv2_done = sem("mv2_done")
        sd2_done = sem("sd2_done")
        rs2_done = sem("rs2_done")
        xn2_done = sem("xn2_done")
        tr2_done = sem("tr2_done")
        xT2_done = sem("xT2_done")
        h_psum = sem("h_psum")
        h_done = sem("h_done")
        hT_psum = sem("hT_psum")
        hT_done = sem("hT_done")
        y_psum = sem("y_psum")
        y_done = sem("y_done")
        ones_set = sem("ones_set")
        xa_in = sem("xa_in")
        v_psum = sem("v_psum")
        v_done = sem("v_done")
        qk_psum = sem("qk_psum")
        qk_done = sem("qk_done")
        s_psum = sem("s_psum")
        max_done = sem("max_done")
        exp_done = sem("exp_done")
        pt_psum = sem("pt_psum")
        pt_even = sem("pt_even")
        pt_odd = sem("pt_odd")
        o_psum = sem("o_psum")
        rs_done = sem("rs_done")
        on_done = sem("on_done")
        oT_psum = sem("oT_psum")
        oT_done = sem("oT_done")
        r_psum = sem("r_psum")
        att_done = sem("att_done")
        added = sem("added")

        block = ctx.enter_context(nc.Block())

        @block.sync
        def _(sp):
            def load_x(k, u):
                sp.dma_start(xin[:, u, :, :].rearrange("p r c -> p (r c)"), x_seg[k]).then_inc(x_in[u], 16)

            load_x(0, 0)
            sp.dma_start(r_w_s[:, :, :], r_w).then_inc(w_rout_in, 16)
            sp.dma_start(r_b_s[:, :], r_b.rearrange("(a e) -> a e", a=1).broadcast_to([P, E])).then_inc(w_rout_in, 16)
            sp.dma_start(halves[:, :], consts).then_inc(const_in, 16)
            for u in range(1, U1):
                load_x(u, u)
            sp.dma_start(b_qk_s[:, :], b_qk).then_inc(const_in, 16)
            for n in range(3):
                sp.dma_start(b1_rep[n * E:(n + 1) * E, :], b1).then_inc(b1_in, 16)
            sp.dma_start(w_in_s[:, :, :], w_in).then_inc(w_attn_in, 16)
            sp.dma_start(w_out_s[:, :, :], w_out).then_inc(w_attn_in, 16)
            sp.dma_start(b_v_s[:, :], b_v.rearrange("(a n) -> a n", a=1).broadcast_to([P, D])).then_inc(w_attn_in, 16)
            sp.dma_start(b_out_s[:, :], b_out.rearrange("(a n) -> a n", a=1).broadcast_to([P, D])).then_inc(w_attn_in, 16)
            with sp.Fori(0, NSEG // U1 - 1) as i:
                for u in range(U1):
                    sp.wait_ge(xn1_done, i * U1 + u + 1)
                    sp.dma_start(xin[:, u, :, :].rearrange("p r c -> p (r c)"),
                                 x_seg[bass.ds(i * U1 + u + U1, 1)].rearrange("a p n -> (a p) n")).then_inc(x_in[u], 16)
            sp.wait_ge(b1_split, 9)
            sp.wait_ge(pool_set, SETUP)
            for n in range(3):
                sp.dma_start(b1_s[n:n + 1, :].rearrange("a (e h) -> a e h", e=E),
                             b1_part[n * E:(n + 1) * E, :]).then_inc(b1_laid, 16)
            sp.dma_start(w1_s[:, :, :], w1).then_inc(w_exp_in, 16)
            sp.dma_start(w2_s[0:HID, :], w2).then_inc(w_exp_in, 16)
            sp.dma_start(w2_s[HID:HID + 1, :], b2.rearrange("(a e) n -> a (e n)", a=1)).then_inc(w_exp_in, 16)
            sp.wait_ge(xTa_done, NSEG)
            def segment_in(i, later):
                if later:
                    sp.wait_ge(v_psum, i)
                    sp.wait_ge(qk_psum, i)
                sp.dma_start(xa[:, :, :].rearrange("p c n -> p (c n)"),
                             xTa[:, bass.ds(i, 1), :, :].rearrange("p a c n -> p (a c n)")).then_inc(xa_in, 16)

            segment_in(0, False)
            with sp.Fori(1, NSEG) as i:
                segment_in(i, True)
        @block.gpsimd
        def _(pool):
            done = [0]

            def step(ins):
                done[0] += 1
                ins.then_inc(pool_set, 1)

            splits = [0]

            def split(ins):
                splits[0] += 1
                ins.then_inc(b1_split, 1)
                pool.wait_ge(b1_split, splits[0])

            step(pool.memset(eps[:, :], EPS))
            step(pool.memset(power[:, :], -0.5))
            step(pool.memset(ident[:, :], 0.0))
            pool.wait_ge(pool_set, 3)
            step(pool.affine_select(out=ident[:, :], in_=ident[:, :], compare_op=ALU.not_equal, fill=1.0,
                                    base=0, pattern=[[-1, P]], channel_multiplier=1))
            step(pool.iota(rank_i[:, :], [[-1, E]], base=E, channel_multiplier=0))
            pool.wait_ge(pool_set, 5)
            step(pool.tensor_copy(rank[:, :], rank_i[:, :]))

            def others():
                step(pool.memset(causal[:, :], 0.0))
                step(pool.memset(before[:, :], 1.0))
                step(pool.memset(onesb[:, :], 1.0))
                step(pool.memset(zeros[:, :], 0.0))
                step(pool.iota(iota_i[:, :], [[1, P]], base=0, channel_multiplier=0))
                step(pool.iota(part_i[:, :], [[0, 1]], base=0, channel_multiplier=1))
                step(pool.iota(tok_i[:, :].rearrange("p (s r) -> p s r", r=R), [[P * R, NSEG], [1, R]], base=1,
                               channel_multiplier=R))
                step(pool.memset(b1_s[:, :], 0.0))
                step(pool.memset(gidx[:, NTILE:NIDX], 0.0))
                step(pool.memset(ends[:, 0:1], 0.0))
                step(pool.memset(v[:, :, :], 1.0))
                pool.wait_ge(pool_set, done[0])
                step(pool.tensor_copy(identb[:, :], ident[:, :]))
                step(pool.affine_select(out=causal[:, :], in_=causal[:, :], compare_op=ALU.is_ge, fill=NEG,
                                        base=0, pattern=[[-1, P]], channel_multiplier=1))
                step(pool.affine_select(out=before[:, :], in_=before[:, :], compare_op=ALU.is_gt, fill=0.0,
                                        base=0, pattern=[[1, P]], channel_multiplier=-1))
                step(pool.tensor_copy(iota[:, :], iota_i[:, :]))
                step(pool.tensor_copy(part[:, :], part_i[:, :]))
                step(pool.tensor_copy(tok1[:, :], tok_i[:, :]))
                pool.wait_ge(b1_in, 48)
                pool.wait_ge(const_in, 32)
                split(pool.tensor_copy(b1_hi[:, :], b1_rep[:, :]))
                split(pool.tensor_tensor(b1_rest[:, :], b1_rep[:, :], b1_hi[:, :], ALU.subtract))
                split(pool.tensor_copy(b1_mid[:, :], b1_rest[:, :]))
                split(pool.tensor_tensor(b1_low[:, :], b1_rest[:, :], b1_mid[:, :], ALU.subtract))
                split(pool.tensor_scalar(b1_sum[:, :], b1_hi[:, :], halves[0:3 * E, 2:3], None, ALU.mult))
                split(pool.tensor_scalar(b1_rest[:, :], b1_mid[:, :], halves[0:3 * E, 3:4], None, ALU.mult))
                split(pool.tensor_tensor(b1_sum[:, :], b1_sum[:, :], b1_rest[:, :], ALU.add))
                split(pool.tensor_scalar(b1_low[:, :], b1_low[:, :], halves[0:3 * E, 4:5], None, ALU.mult))
                split(pool.tensor_tensor(b1_part[:, :], b1_sum[:, :], b1_low[:, :], ALU.add))

            others()
            assert done[0] == SETUP
            def router_steps(i, later):
                for u in range(U1):
                    k = i * U1 + u
                    pool.wait_ge(mv1_done, k + 1)
                    pool.tensor_tensor(sd1[:, u, :], mv1[:, u, :, 1], eps[:, :], ALU.add).then_inc(sd1_done, 1)
                    pool.wait_ge(sd1_done, k + 1)
                    pool.tensor_tensor(rs1[:, u, :], sd1[:, u, :], power[:, :], ALU.pow).then_inc(rs1_done, 1)
                    pool.wait_ge(rs1_done, k + 1)
                    if later or u >= 2:
                        pool.wait_ge(tr1_done, k - 1)
                    pool.sem_inc(passed_pool, 1)
                    for r in range(R):
                        last = pool.tensor_scalar(xn1[:, u % 2, r, :], xin[:, u, r, :], mv1[:, u, r, 0:1],
                                                  rs1[:, u, r:r + 1], ALU.subtract, ALU.mult)
                    last.then_inc(xn1_done, 1)

            router_steps(0, False)
            with pool.Fori(1, NSEG // U1) as i:
                router_steps(i, True)
            pool.wait_ge(pos_done, 1)
            def list_steps(i, later):
                for u in range(2):
                    n = i * 2 + u
                    if later:
                        pool.wait_ge(list_mm, n - 1)
                    pool.tensor_copy(slot_col[:, u, :], slot_f[:, bass.ds(n * 4, 4)]).then_inc(slot_set, 1)
                    pool.wait_ge(slot_set, n + 1)
                    pool.sem_inc(passed_pool, 1)
                    for m in range(4):
                        last = pool.tensor_scalar(at_slot[:, u, m, :], iota[:, :], slot_col[:, u, m:m + 1], None,
                                                  ALU.is_equal)
                    last.then_inc(slot_oh, 1)

            list_steps(0, False)
            with pool.Fori(1, T // 8) as i:
                list_steps(i, True)
            def gather(s, n):
                for t in range(2):
                    pool.indirect_dma_start(out=xg[:, s, t, :], out_offset=None, in_=x_rows[:, :],
                                            in_offset=bass.IndirectOffsetOnAxis(ap=gcol[:, s, t:t + 1], axis=0))\
                        .then_inc(gathered[s], 16)

            pool.wait_ge(idx_done, 1)
            for s in range(SLOTS):
                pool.tensor_copy(gcol[:, s, :], gidx[:, 2 * s:2 * s + 2]).then_inc(gcol_set, 1)
            pool.wait_ge(gcol_set, SLOTS)
            for s in range(SLOTS):
                gather(s, s)
            pool.wait_ge(mv2_done, 1)
            pool.tensor_tensor(sd2[:, 0, :], mv2[:, 0, :, 1], eps[:, 0:2], ALU.add).then_inc(sd2_done, 1)
            pool.wait_ge(sd2_done, 1)
            pool.tensor_tensor(rs2[:, 0, :], sd2[:, 0, :], power[:, 0:2], ALU.pow).then_inc(rs2_done, 1)
            def loop_step(i, later):
                for s in range(SLOTS):
                    n = i * SLOTS + s
                    s1 = (s + 1) % SLOTS
                    pool.wait_ge(mv2_done, n + 2)
                    pool.tensor_tensor(sd2[:, s1, :], mv2[:, s1, :, 1], eps[:, 0:2], ALU.add).then_inc(sd2_done, 1)
                    pool.wait_ge(sd2_done, n + 2)
                    pool.tensor_tensor(rs2[:, s1, :], sd2[:, s1, :], power[:, 0:2], ALU.pow).then_inc(rs2_done, 1)
                    if later:
                        pool.wait_ge(scattered[s], i * 32)
                    pool.tensor_copy(scol[:, s, :], sidx[:, bass.ds(n * 2, 2)]).then_inc(scol_set, 1)
                    pool.wait_ge(gathered[s], i * 32 + 32)
                    pool.tensor_copy(gcol[:, s, :], gidx[:, bass.ds(n * 2 + 2 * SLOTS, 2)]).then_inc(gcol_set, 1)
                    pool.wait_ge(scol_set, n + 1)
                    pool.wait_ge(gcol_set, n + 1 + SLOTS)
                    pool.wait_ge(y_done, n + 1)
                    pool.sem_inc(passed_pool, 1)
                    for t in range(2):
                        pool.indirect_dma_start(out=out_rows[:, :],
                                                out_offset=bass.IndirectOffsetOnAxis(ap=scol[:, s, t:t + 1], axis=0),
                                                in_=yb[:, s, t, :], in_offset=None, bounds_check=NTOK - 1,
                                                oob_is_err=False).then_inc(scattered[s], 16)
                    gather(s, n)

            loop_step(0, False)
            with pool.Fori(1, NSEG) as i:
                loop_step(i, True)
            for s in range(SLOTS):
                pool.wait_ge(scattered[s], 32 * NSEG)
                pool.wait_ge(gathered[s], 32 * NSEG + 32)
            pool.wait_ge(att_done, NSEG)
            pool.dma_start(att_rows, att[:, :, :], accum_op=ALU.add).then_inc(added, 16)
            pool.wait_ge(added, 16)

        @block.vector
        def _(dve):
            dve.wait_ge(pool_set, 6)
            dve.wait_ge(w_rout_in, 32)
            def router_steps(i, later):
                for u in range(U1):
                    k = i * U1 + u
                    dve.wait_ge(x_in[u], i * 16 + 16)
                    for r in range(R):
                        last = dve.bn_stats(st1[:, r, :], xin[:, u, r, :])
                    last.then_inc(st1_done, 1)
                    dve.wait_ge(st1_done, k + 1)
                    dve.sem_inc(passed_dve, 1)
                    for r in range(R):
                        last = dve.bn_aggr(mv1[:, u, r, :], st1[:, r, :])
                    last.then_inc(mv1_done, 1)
                    dve.wait_ge(lg_psum, k + 1)
                    dve.tensor_tensor(lg[:, :, :], bank[4][:, 0:R * E].rearrange("p (r e) -> p r e", r=R),
                                      r_b_s[:, None, :].broadcast_to([P, R, E]), ALU.add).then_inc(lg_done, 1)
                    dve.wait_ge(lg_done, k + 1)
                    dve.reduce_max(lmax[:, :], lg[:, :, :], AX.X).then_inc(rt_step, 1)
                    dve.wait_ge(rt_step, k * 4 + 1)
                    dve.tensor_tensor(hit[:, :, :], lg[:, :, :], lmax[:, :, None].broadcast_to([P, R, E]),
                                      ALU.is_equal).then_inc(rt_step, 1)
                    dve.wait_ge(rt_step, k * 4 + 2)
                    dve.tensor_tensor(hit[:, :, :], hit[:, :, :], rank[:, None, :].broadcast_to([P, R, E]),
                                      ALU.mult).then_inc(rt_step, 1)
                    dve.wait_ge(rt_step, k * 4 + 3)
                    dve.reduce_max(first[:, :], hit[:, :, :], AX.X).then_inc(rt_step, 1)
                    dve.wait_ge(rt_step, k * 4 + 4)
                    dve.tensor_tensor(onehot[:, :, bass.ds(k * R, R)].rearrange("p e r -> p r e"),
                                      rank[:, None, :].broadcast_to([P, R, E]),
                                      first[:, :, None].broadcast_to([P, R, E]), ALU.is_equal).then_inc(oh_done, 1)

            router_steps(0, False)
            with dve.Fori(1, NSEG // U1) as i:
                router_steps(i, True)
            steps = [0]

            def step(ins):
                steps[0] += 1
                ins.then_inc(dsp, 1)
                dve.wait_ge(dsp, steps[0])

            dve.wait_ge(pool_set, SETUP)
            dve.wait_ge(oh_done, NSEG)
            oh_flat = onehot[:, :, :].rearrange("p e t -> p (e t)")
            step(dve.tensor_tensor_scan(count[:, :, :].rearrange("p e t -> p (e t)"), oh_flat, oh_flat, 0.0,
                                        ALU.add, ALU.max))
            step(dve.tensor_copy(ends[:, 1:E + 1], count[:, :, T - 1]))
            dve.tensor_tensor(rowtot[:, :], ends[:, 1:E + 1], ends[:, 0:E], ALU.subtract).then_inc(tot_ready, 1)
            dve.wait_ge(tot_psum, 1)
            step(dve.tensor_scalar(cnt_i[:, :], bank[0][:, E:2 * E], float(P - 1), None, ALU.add))
            step(dve.tensor_scalar(til_i[:, :], cnt_i[:, :], 7, None, ALU.arith_shift_right))
            step(dve.tensor_copy(til[:, :], til_i[:, :]))
            step(dve.tensor_tensor_scan(cum[:, :], til[:, :], til[:, :], 0.0, ALU.add, ALU.max))
            step(dve.tensor_scalar(past[:, :], cum[:, :], part[:, 0:1], None, ALU.is_le))
            step(dve.reduce_sum(te0[:, :], past[:, :], AX.X))
            dve.tensor_scalar(te1[:, :], te0[:, :], float(E - 1), None, ALU.min).then_inc(te_ready, 1)
            step(dve.tensor_tensor(offs[:, :], cum[:, :], til[:, :], ALU.subtract))
            step(dve.scalar_tensor_tensor(base0[:, :], offs[:, :], float(P), bank[0][:, 0:E], ALU.mult, ALU.add))
            step(dve.scalar_tensor_tensor(base[:, :], base0[:, :], -1.0, ends[:, 0:E], ALU.add, ALU.subtract))
            step(dve.tensor_tensor(place[:, :, :], count[:, :, :], base[:, :, None].broadcast_to([P, E, T]), ALU.add))
            step(dve.tensor_tensor(place[:, :, :], place[:, :, :], onehot[:, :, :], ALU.mult))
            step(dve.reduce_sum(pos[:, :], place[:, :, :].rearrange("p e t -> p t e"), AX.X))
            step(dve.tensor_copy(pos_i[:, :], pos[:, :]))
            dve.tensor_scalar(slot_i[:, :], pos_i[:, :], P - 1, None, ALU.bitwise_and)
            step(dve.tensor_scalar(tile_i[:, :], pos_i[:, :], 7, None, ALU.arith_shift_right))
            dve.tensor_copy(slot_f[:, :], slot_i[:, :]).then_inc(pos_done, 1)
            step(dve.tensor_copy(tile_f[:, :], tile_i[:, :]))
            dve.wait_ge(te_psum, 1)
            dve.tensor_copy(te_i[0:1, :], bank[1][0:1, 0:P]).then_inc(te_done, 1)
            def list_steps(i, later):
                for u in range(2):
                    n = i * 2 + u
                    if later:
                        dve.wait_ge(list_mm, n - 1)
                    for m in range(4):
                        last = dve.tensor_scalar(tok_at[:, u, m, :], iota[:, 0:NTILE],
                                                 tile_f[:, bass.ds(n * 4 + m, 1)], tok1[:, bass.ds(n * 4 + m, 1)],
                                                 ALU.is_equal, ALU.mult)
                    last.then_inc(tok_done, 1)

            list_steps(0, False)
            with dve.Fori(1, T // 8) as i:
                list_steps(i, True)
            dve.wait_ge(list_mm, T // 4 + 1)
            dve.tensor_scalar(gidx[:, 0:NTILE], bank[2][:, 0:NTILE], -1.0, 0.0, ALU.add, ALU.max)
            step(dve.tensor_scalar(empty[:, :], bank[2][:, 0:NTILE], 0.0, FAR, ALU.is_equal, ALU.mult))
            dve.scalar_tensor_tensor(sidx[:, :], bank[2][:, 0:NTILE], -1.0, empty[:, :], ALU.add, ALU.add)\
                .then_inc(idx_done, 1)
            dve.memset(hT[HID:HID + 1, :, :], 1.0).then_inc(ones_set, 1)

            def stats(s, n, turn):
                dve.wait_ge(gathered[s], turn * 32 + 32)
                for t in range(2):
                    last = dve.bn_stats(st2[:, t, :], xg[:, s, t, :])
                last.then_inc(st2_done, 1)
                dve.wait_ge(st2_done, n + 1)
                dve.sem_inc(passed_dve, 1)
                for t in range(2):
                    last = dve.bn_aggr(mv2[:, s, t, :], st2[:, t, :])
                last.then_inc(mv2_done, 1)

            def normalise(s, n):
                dve.wait_ge(rs2_done, n + 1)
                for t in range(2):
                    last = dve.tensor_scalar(xn2[:, s, t, :], xg[:, s, t, :], mv2[:, s, t, 0:1], rs2[:, s, t:t + 1],
                                             ALU.subtract, ALU.mult)
                last.then_inc(xn2_done, 1)

            def relu_hidden(n):
                dve.wait_ge(h_psum, n + 1)
                dve.tensor_scalar(hid[:, :, :], b_h[:, 0:2 * HID].rearrange("p (t h) -> p t h", t=2), 0.0, None,
                                  ALU.max).then_inc(h_done, 1)

            def sums(s, n, i, later):
                dve.wait_ge(y_psum, n + 1)
                if later:
                    dve.wait_ge(scattered[s], i * 32)
                dve.scalar_tensor_tensor(yb[:, s, :, :].rearrange("p t c -> p (t c)"), b_y[:, :], 0.0,
                                         xg[:, s, :, :].rearrange("p t c -> p (t c)"), ALU.max, ALU.add)\
                    .then_inc(y_done, 1)

            def turn_probs(j, i):
                dve.wait_ge(pt_psum, i * BANKS + j + 1)
                dve.tensor_copy(probsT[:, 4 * j:4 * j + 4, :].rearrange("p n k -> p (n k)"), bank[j][:, :])\
                    .then_inc(pt_even, 1)

            def norm_out(i):
                dve.wait_ge(o_psum, i)
                o = b_att[:, 0:NH * (DH + 1)].rearrange("p (h d) -> p h d", h=NH)
                dve.reciprocal(rsum[:, :], o[:, :, DH]).then_inc(rs_done, 1)
                dve.wait_ge(rs_done, i)
                dve.tensor_tensor(on[:, :, :], o[:, :, 0:DH], rsum[:, :, None].broadcast_to([P, NH, DH]), ALU.mult)\
                    .then_inc(on_done, 1)

            def bias_out(i):
                dve.wait_ge(r_psum, i)
                dve.tensor_tensor(att[:, bass.ds(i - 1, 1), :].rearrange("p a c -> p (a c)"), b_att[:, 0:D],
                                  b_out_s[:, :], ALU.add).then_inc(att_done, 1)

            stats(0, 0, 0)
            normalise(0, 0)
            dve.wait_ge(w_attn_in, 64)
            def loop_step(i, later):
                n = i * SLOTS
                stats(1, n + 1, i)
                relu_hidden(n)
                if later:
                    norm_out(i)
                normalise(1, n + 1)
                sums(0, n, i, later)
                if later:
                    bias_out(i)
                stats(2, n + 2, i)
                dve.wait_ge(v_psum, i + 1)
                dve.tensor_tensor(v[:, :, 0:DH], b_att[:, 0:D].rearrange("p (h d) -> p h d", h=NH),
                                  b_v_s[:, :].rearrange("p (h d) -> p h d", h=NH), ALU.add).then_inc(v_done, 1)
                relu_hidden(n + 1)
                normalise(2, n + 2)
                sums(1, n + 1, i, later)
                for j in range(BANKS):
                    dve.wait_ge(s_psum, i * BANKS + j + 1)
                    dve.tensor_reduce(nmax[:, 4 * j:4 * j + 4], bank[j][:, :].rearrange("p (n k) -> p n k", n=4),
                                      AX.X, ALU.max, negate=True).then_inc(max_done, 1)
                stats(0, n + 3, i + 1)
                relu_hidden(n + 2)
                turn_probs(0, i)
                normalise(0, n + 3)
                sums(2, n + 2, i, later)
                turn_probs(2, i)

            loop_step(0, False)
            with dve.Fori(1, NSEG) as i:
                loop_step(i, True)
            norm_out(NSEG)
            bias_out(NSEG)

        @block.scalar
        def _(act):
            with act.Fori(0, NSEG // U1) as i:
                for u in range(U1):
                    k = i * U1 + u
                    act.wait_ge(tr1_done, k + 1)
                    for c in range(C):
                        last = act.activation(xT1[:, u % 2, c, :, :].rearrange("p r n -> p (r n)"),
                                              bank[2 * (u % 2) + c][:, :], ACT.Copy)
                    last.then_inc(xT1_done, 1)
                    act.wait_ge(xT1_done, k + 1)
                    act.activation(xTa[:, bass.ds(k, 1), :, :].rearrange("p a c n -> p (a c) n"),
                                   xT1[:, u % 2, :, 0, :], ACT.Copy).then_inc(xTa_done, 1)
            act.wait_ge(const_in, 32)
            for c in range(C):
                act.activation(q_bias[:, c:c + 1], b_qk_s[:, c:c + 1], ACT.Copy, scale=DH ** -0.5)
                for m in range(2):
                    last = act.activation(k_bias[:, c, m:m + 1], b_qk_s[:, C + c:C + c + 1], ACT.Copy,
                                          scale=halves[:, m:m + 1])
            last.then_inc(bias_made, 1)

            def turn_probs(j, i):
                act.wait_ge(pt_psum, i * BANKS + j + 1)
                act.activation(probsT[:, 4 * j:4 * j + 4, :].rearrange("p n k -> p (n k)"), bank[j][:, :], ACT.Copy)\
                    .then_inc(pt_odd, 1)

            def turn_x(n):
                act.wait_ge(tr2_done, n + 1)
                act.activation(xT2[:, :, :, :].rearrange("p c t n -> p (c t n)"), b_xT[:, :], ACT.Copy)\
                    .then_inc(xT2_done, 1)

            def turn_hidden(n):
                act.wait_ge(hT_psum, n + 1)
                act.activation(hT[0:HID, :, :].rearrange("p t n -> p (t n)"), b_h[0:HID, P:P + 2 * P], ACT.Copy)\
                    .then_inc(hT_done, 1)

            def turn_out(i):
                act.wait_ge(oT_psum, i)
                act.activation(oT[:, :, :].rearrange("p c n -> p (c n)"), b_att[:, 0:D], ACT.Copy).then_inc(oT_done, 1)

            def exps(j, i):
                act.wait_ge(max_done, i * BANKS + j + 1)
                for m in range(4):
                    last = act.activation(probs[:, 4 * j + m, :], bank[j][:, m * P:(m + 1) * P], ACT.Exp,
                                          bias=nmax[:, 4 * j + m:4 * j + m + 1])
                last.then_inc(exp_done, 1)

            act.wait_ge(bias_made, 1)
            act.wait_ge(idx_done, 1)
            def loop_step(i, later):
                n = i * SLOTS
                turn_x(n)
                turn_hidden(n)
                if later:
                    turn_out(i)
                turn_x(n + 1)
                act.wait_ge(qk_psum, i + 1)
                for c in range(C):
                    act.activation(qT[:, c, :], b_att[:, c * P:(c + 1) * P], ACT.Identity, scale=DH ** -0.5,
                                   bias=q_bias[:, c:c + 1])
                    for m in range(2):
                        last = act.activation(kT[:, c, m, :], b_att[:, (C + c) * P:(C + c + 1) * P], ACT.Identity,
                                              scale=halves[:, m:m + 1], bias=k_bias[:, c, m:m + 1])
                last.then_inc(qk_done, 1)
                turn_hidden(n + 1)
                exps(0, i)
                turn_x(n + 2)
                exps(1, i)
                turn_hidden(n + 2)
                exps(2, i)
                turn_probs(1, i)
                exps(3, i)
                turn_probs(3, i)

            loop_step(0, False)
            with act.Fori(1, NSEG) as i:
                loop_step(i, True)
            turn_out(NSEG)

        @block.tensor
        def _(pe):
            pe.wait_ge(pool_set, 6)
            pe.wait_ge(w_rout_in, 32)
            def router_steps(i, later):
                for u in range(U1):
                    k = i * U1 + u
                    pe.wait_ge(xn1_done, k + 1)
                    for c in range(C):
                        for r in range(R):
                            last = pe.transpose(bank[2 * (u % 2) + c][:, r * P:(r + 1) * P],
                                                xn1[:, u % 2, r, c * P:(c + 1) * P], ident[:, :])
                    last.then_inc(tr1_done, 1)
                    pe.wait_ge(xT1_done, k + 1)
                    if later or u:
                        pe.wait_ge(lg_done, k)
                    for r in range(R):
                        for c in range(C):
                            last = pe.matmul(bank[4][:, r * E:(r + 1) * E], xT1[:, u % 2, c, r, :],
                                             r_w_s[:, c, :], start=(c == 0), stop=(c == C - 1))
                    last.then_inc(lg_psum, 1)

            router_steps(0, False)
            with pe.Fori(1, NSEG // U1) as i:
                router_steps(i, True)
            pe.wait_ge(tot_ready, 1)
            pe.wait_ge(pool_set, SETUP)
            pe.matmul(bank[0][:, 0:E], before[:, :], rowtot[:, :], start=True, stop=True)
            pe.matmul(bank[0][:, E:2 * E], onesb[:, :], rowtot[:, :], start=True, stop=True).then_inc(tot_psum, 1)
            pe.wait_ge(te_ready, 1)
            pe.matmul(bank[1][0:1, 0:P], te1[:, 0:1], ident[:, :], start=True, stop=True).then_inc(te_psum, 1)
            pe.matmul(bank[2][:, 0:NTILE], onesb[:, :], zeros[:, :], start=True, stop=False)
            def list_steps(i, later):
                for u in range(2):
                    n = i * 2 + u
                    pe.wait_ge(slot_oh, n + 1)
                    pe.wait_ge(tok_done, n + 1)
                    for m in range(4):
                        last = pe.matmul(bank[2][:, 0:NTILE], at_slot[:, u, m, :], tok_at[:, u, m, :],
                                         start=False, stop=False)
                    last.then_inc(list_mm, 1)

            list_steps(0, False)
            with pe.Fori(1, T // 8) as i:
                list_steps(i, True)
            pe.matmul(bank[2][:, 0:NTILE], onesb[:, :], zeros[:, :], start=False, stop=True).then_inc(list_mm, 1)

            def turn_x(s, n, later):
                pe.wait_ge(xn2_done, n + 1)
                if later:
                    pe.wait_ge(xT2_done, n)
                for c in range(C):
                    for t in range(2):
                        last = pe.transpose(b_xT[:, (2 * c + t) * P:(2 * c + t + 1) * P],
                                            xn2[:, s, t, c * P:(c + 1) * P], ident[:, :])
                last.then_inc(tr2_done, 1)

            def hidden(n, experts, later):
                pe.wait_ge(xT2_done, n + 1)
                if later:
                    pe.wait_ge(hT_done, n)
                for t in range(2):
                    o = b_h[:, t * HID:(t + 1) * HID]
                    at = bass.ds(experts[t] * HID, HID)
                    pe.matmul(o, onesb[:, :], b1_s[:, at], start=True, stop=False)
                    for c in range(C):
                        last = pe.matmul(o, xT2[:, c, t, :], w1_s[:, c, at], start=False, stop=(c == C - 1))
                last.then_inc(h_psum, 1)

            def turn_hidden(n):
                pe.wait_ge(h_done, n + 1)
                pe.sem_inc(passed_pe, 1)
                for t in range(2):
                    last = pe.transpose(b_h[0:HID, (1 + t) * P:(2 + t) * P], hid[:, t, :], ident[:, :])
                last.then_inc(hT_psum, 1)

            def outputs(n, experts, later):
                pe.wait_ge(hT_done, n + 1)
                if later:
                    pe.wait_ge(y_done, n)
                for t in range(2):
                    last = pe.matmul(b_y[:, t * D:(t + 1) * D], hT[:, t, :], w2_s[:, bass.ds(experts[t] * D, D)],
                                     start=True, stop=True)
                last.then_inc(y_psum, 1)

            def attend(i):
                pe.wait_ge(pt_even, i * 2)
                pe.wait_ge(pt_odd, i * 2)
                pe.wait_ge(v_done, i)
                pe.wait_ge(qk_done, i)
                for j in range(BANKS):
                    for m in range(4):
                        h = head_of(j, m)
                        last = pe.matmul(b_att[:, h * (DH + 1):(h + 1) * (DH + 1)], probsT[:, 4 * j + m, :],
                                         v[:, h, :], start=True, stop=True)
                last.then_inc(o_psum, 1)

            def turn_out(i):
                pe.wait_ge(on_done, i)
                flat = on[:, :, :].rearrange("p h d -> p (h d)")
                for c in range(C):
                    last = pe.transpose(b_att[:, c * P:(c + 1) * P], flat[:, c * P:(c + 1) * P], ident[:, :])
                last.then_inc(oT_psum, 1)

            def project(i):
                pe.wait_ge(oT_done, i)
                for c in range(C):
                    last = pe.matmul(b_att[:, 0:D], oT[:, c, :], w_out_s[:, c, :], start=(c == 0), stop=(c == C - 1))
                last.then_inc(r_psum, 1)

            def values(i, later):
                pe.wait_ge(xa_in, i * 16 + 16)
                if later:
                    pe.wait_ge(att_done, i)
                for c in range(C):
                    last = pe.matmul(b_att[:, 0:D], xa[:, c, :], w_in_s[:, c, 2 * D:3 * D], start=(c == 0),
                                     stop=(c == C - 1))
                last.then_inc(v_psum, 1)

            def queries_keys(i):
                pe.wait_ge(v_done, i + 1)
                for g in range(2 * C):
                    for c in range(C):
                        last = pe.matmul(b_att[:, g * P:(g + 1) * P], w_in_s[:, c, g * P:(g + 1) * P], xa[:, c, :],
                                         start=(c == 0), stop=(c == C - 1))
                last.then_inc(qk_psum, 1)

            def scores(i, later):
                pe.wait_ge(qk_done, i + 1)
                if later:
                    pe.wait_ge(pt_even, i * 2)
                    pe.wait_ge(pt_odd, i * 2)
                for j in range(BANKS):
                    for m in range(4):
                        pe.matmul(bank[j][:, m * P:(m + 1) * P], identb[:, :], causal[:, :], start=(m == 0),
                                  stop=False, skip_group_check=True)
                for g in range(C):
                    for j in range(BANKS):
                        rows = slice(32 * j, 32 * j + 32)
                        last = pe.matmul(bank[j][:, g * 2 * P:(g + 1) * 2 * P], qT[rows, g, :],
                                         kT[rows, g, :, :].rearrange("p m n -> p (m n)"), start=False,
                                         stop=(g == C - 1), skip_group_check=True)
                        if g == C - 1:
                            last.then_inc(s_psum, 1)

            def turn_probs(j, i):
                pe.wait_ge(exp_done, i * BANKS + j + 1)
                for m in range(4):
                    last = pe.transpose(bank[j][:, m * P:(m + 1) * P], probs[:, 4 * j + m, :], ident[:, :])
                last.then_inc(pt_psum, 1)

            pe.wait_ge(te_done, 1)
            pe.wait_ge(idx_done, 1)
            pe.wait_ge(ones_set, 1)
            pe.wait_ge(b1_laid, 48)
            pe.wait_ge(w_exp_in, 48)
            pe.wait_ge(w_attn_in, 64)
            def loop_step(i, later):
                n = i * SLOTS
                experts = [pe.value_load(te_i[0:1, bass.ds(i * 2 * SLOTS + m, 1)], min_val=0, max_val=E - 1)
                           for m in range(2 * SLOTS)]
                turn_x(0, n, later)
                if later:
                    attend(i)
                hidden(n, experts[0:2], later)
                turn_hidden(n)
                if later:
                    turn_out(i)
                outputs(n, experts[0:2], later)
                if later:
                    project(i)

                turn_x(1, n + 1, True)
                values(i, later)
                hidden(n + 1, experts[2:4], True)
                queries_keys(i)
                turn_hidden(n + 1)
                outputs(n + 1, experts[2:4], True)
                scores(i, later)

                turn_x(2, n + 2, True)
                hidden(n + 2, experts[4:6], True)
                turn_probs(0, i)
                turn_hidden(n + 2)
                turn_probs(1, i)
                outputs(n + 2, experts[4:6], True)
                turn_probs(2, i)
                turn_probs(3, i)

            loop_step(0, False)
            with pe.Fori(1, NSEG) as i:
                loop_step(i, True)
            attend(NSEG)
            turn_out(NSEG)
            project(NSEG)


def kernel(L0_attn_x, L0_attn_w_in, L0_attn_b_in, L0_attn_w_out, L0_attn_b_out, L0_ffn_router_w, L0_ffn_router_b,
           L0_ffn_weights1, L0_ffn_bias1, L0_ffn_weights2, L0_ffn_bias2):
    import concourse.bacc as bacc
    import numpy as np
    from concourse.bass_utils import run_bass_kernel_spmd

    def rows(a):
        a = np.asarray(a)
        return np.ascontiguousarray(a.reshape(C, P, a.shape[1]).transpose(1, 0, 2))

    b_in = np.asarray(L0_attn_b_in)
    w1 = np.asarray(L0_ffn_weights1).reshape(E, C, P, HID).transpose(2, 1, 0, 3)
    w2 = np.asarray(L0_ffn_weights2).transpose(1, 0, 2)
    row = np.arange(P)
    consts = np.stack([row // DH % 2 == 0, row // DH % 2 == 1] + [row // E == n for n in range(3)], axis=1)
    arrays = {
        "x": np.asarray(L0_attn_x),
        "consts": consts.astype(np.float32),
        "w_in": rows(np.asarray(L0_attn_w_in).T),
        "b_qk": np.ascontiguousarray(b_in[:2 * D].reshape(2 * C, P).T),
        "b_v": np.ascontiguousarray(b_in[2 * D:]),
        "w_out": rows(np.asarray(L0_attn_w_out).T),
        "b_out": np.asarray(L0_attn_b_out),
        "r_w": rows(np.asarray(L0_ffn_router_w).T),
        "r_b": np.asarray(L0_ffn_router_b),
        "w1": np.ascontiguousarray(w1).reshape(P, C, E * HID),
        "b1": np.asarray(L0_ffn_bias1),
        "w2": np.ascontiguousarray(w2).reshape(HID, E * D),
        "b2": np.asarray(L0_ffn_bias2),
    }
    nc = bacc.Bacc("TRN2", target_bir_lowering=False, num_devices=1)
    args = [nc.dram_tensor(f"in_{name}", a.shape, mybir.dt.from_np(a.dtype), kind="ExternalInput").ap()
            for name, a in arrays.items()]
    out = nc.dram_tensor("out", arrays["x"].shape, FP32, kind="ExternalOutput").ap()
    build(nc, *args, out)
    r = run_bass_kernel_spmd(nc, [{f"in_{name}": a for name, a in arrays.items()}], core_ids=[0])
    return r.results[0]["out"]
```

```python
from contextlib import ExitStack

import concourse.bass as bass
from concourse import mybir

FP32 = mybir.dt.float32
BF16 = mybir.dt.bfloat16
I32 = mybir.dt.int32
ALU = mybir.AluOpType
ACT = mybir.ActivationFunctionType
AX = mybir.AxisListType

P = 128
D = 256
C = D // P
R = 4
NSEG = 16
NTOK = NSEG * P * R
NH = 16
DH = D // NH
E = 32
HID = D // 4
T = NTOK // P
SLOTS = 3
NPAIR = NSEG * SLOTS
NTILE = 2 * NPAIR
NIDX = NTILE + 2 * SLOTS
U1 = 4
BANKS = 4
SETUP = 23
NEG = -1e9
ROW = D + 2
HS = 32
FAR = 1048576.0
EPS = 1e-5
assert NTILE >= T + E - 1


def build(nc, x, consts, w_in, b_qk, b_v, w_out, b_out, r_w, r_b, w1, w2, out):
    ctx = ExitStack()
    with ctx:
        def sb(name, shape, dt=FP32):
            return ctx.enter_context(nc.sbuf_tensor(name, shape, dt))

        def sem(name):
            return ctx.enter_context(nc.semaphore(name))

        ident = sb("ident", [P, P])
        identb = sb("identb", [P, P], BF16)
        causal = sb("causal", [P, P], BF16)
        before = sb("before", [P, P], BF16)
        onesb = sb("onesb", [P, P], BF16)
        zeros = sb("zeros", [P, 2 * NTILE], BF16)
        iota_i = sb("iota_i", [P, P], I32)
        iota = sb("iota", [P, P], BF16)
        part_i = sb("part_i", [P, 1], I32)
        part = sb("part", [P, 1])
        rank_i = sb("rank_i", [P, E], I32)
        rank = sb("rank", [P, E])
        tok_i = sb("tok_i", [P, T], I32)
        tok_hi = sb("tok_hi", [P, T], I32)
        tok_lo = sb("tok_lo", [P, T], I32)
        tok_parts = sb("tok_parts", [P, T, 2], BF16)
        heads8 = sb("heads8", [P, 8])
        eps = sb("eps", [P, 4])
        power = sb("power", [P, 4])
        zero4 = sb("zero4", [P, 4])
        warm = sb("warm", [P, 4])
        w_in_s = sb("w_in_s", [P, C, 3 * D])
        b_qk_s = sb("b_qk_s", [P, 2 * C])
        q_bias = sb("q_bias", [P, C])
        b_v_s = sb("b_v_s", [P, D])
        w_out_s = sb("w_out_s", [P, C, D])
        b_out_s = sb("b_out_s", [P, D])
        r_w_s = sb("r_w_s", [P, C, E])
        r_b_s = sb("r_b_s", [E, 1])
        w1_s = sb("w1_s", [P, E, C * HID])
        w2_s = sb("w2_s", [HID + 1, E, D + 1])
        xin = sb("xin", [P, U1, R, ROW])
        st1 = sb("st1", [P, 2, R, 6])
        sd1 = sb("sd1", [P, R])
        ms1 = sb("ms1", [P, R])
        nb1 = sb("nb1", [P, U1, R])
        xn1 = sb("xn1", [P, 2, R, D])
        xT1 = sb("xT1", [P, 2, C, R, P])
        xTa = sb("xTa", [P, NSEG, C, P])
        lgT = sb("lgT", [E, 2, R * P])
        lg = sb("lg", [P, U1 * R, E])
        lmax = sb("lmax", [P, U1 * R])
        hit = sb("hit", [P, U1 * R, E])
        first = sb("first", [P, U1 * R])
        onehot = sb("onehot", [P, E, T])
        count = sb("count", [P, E, T])
        place = sb("place", [P, E, T])
        ends = sb("ends", [P, E + 1])
        rowtot = sb("rowtot", [P, E], BF16)
        cnt_i = sb("cnt_i", [P, E], I32)
        til_i = sb("til_i", [P, E], I32)
        til = sb("til", [P, E])
        cum = sb("cum", [P, E])
        offs = sb("offs", [P, E])
        base0 = sb("base0", [P, E])
        base = sb("base", [P, E])
        past = sb("past", [P, E])
        te0 = sb("te0", [P, 1])
        te1 = sb("te1", [P, 1])
        te_i = sb("te_i", [1, P], I32)
        pos = sb("pos", [P, T])
        pos_i = sb("pos_i", [P, T], I32)
        tile_i = sb("tile_i", [P, T], I32)
        slot_i = sb("slot_i", [P, T], I32)
        slot_b = sb("slot_b", [P, T], BF16)
        tile_b = sb("tile_b", [P, T], BF16)
        at_slot = sb("at_slot", [P, 2, 4, P], BF16)
        at_tile = sb("at_tile", [P, 2, 4, NTILE], BF16)
        tok_at = sb("tok_at", [P, 2, 4, 2, NTILE], BF16)
        listed = sb("listed", [P, NTILE])
        empty = sb("empty", [P, NTILE])
        gidx = sb("gidx", [P, NIDX], I32)
        sidx = sb("sidx", [P, NTILE], I32)
        gcol = sb("gcol", [P, SLOTS, 2], I32)
        scol = sb("scol", [P, SLOTS, 2], I32)
        xg = sb("xg", [P, SLOTS, 2, ROW])
        xT2 = sb("xT2", [P, C, 2, P])
        w1_now = sb("w1_now", [P, SLOTS, 2, C * HID])
        w2_now = sb("w2_now", [HID + 1, SLOTS, 2, D + 1])
        hT = sb("hT", [HID + 1, 2, P])
        yb = sb("yb", [P, SLOTS, 2, D])
        xa = sb("xa", [P, C, P])
        qT = sb("qT", [P, C, P])
        v = sb("v", [P, NH, HS])
        nmax = sb("nmax", [P, NH])
        rsum = sb("rsum", [P, NH])
        oraw = sb("oraw", [P, 4 * P])
        on = sb("on", [P, NH, DH])
        oT = sb("oT", [P, C, P])
        att = sb("att", [P, NSEG, D])
        xn2 = xT1[:, :, :, :, :].rearrange("p u c r n -> p (u c r n)")[:, 0:SLOTS * 2 * D]\
            .rearrange("p (s t c) -> p s t c", s=SLOTS, t=2)
        kT = onehot[:, :, :].rearrange("p e t -> p (e t)").rearrange("p (c m n) -> p c m n", c=C, m=8)
        probs = count[:, :, :].rearrange("p e t -> p (e t)").rearrange("p (n k) -> p n k", k=P)
        probsT = place[:, :, :].rearrange("p e t -> p (e t)").rearrange("p (n k) -> p n k", k=P)

        bank = [ctx.enter_context(nc.psum_tensor(f"bank{i}", [P, 512], FP32)) for i in range(8)]
        b_o, b_v_k, b_x, b_y = bank[4], bank[6], bank[5], bank[7]

        x_seg = x.rearrange("b (s p r) c -> (b s) p (r c)", p=P, r=R)
        out_rows = out.rearrange("b n c -> (b n) c")
        rows = nc.dram_tensor("rows", [NTOK, ROW], FP32, kind="Internal").ap()
        rows_seg = rows.rearrange("(s p r) c -> s p (r c)", p=P, r=R)
        att_rows = out.rearrange("b (s p r) c -> p (b s) r c", p=P, r=R)[:, :, 0, :]

        passed_dve = sem("passed_dve")
        passed_pe = sem("passed_pe")
        passed_pool = sem("passed_pool")
        pool_set = sem("pool_set")
        const_in = sem("const_in")
        w_attn_in = sem("w_attn_in")
        w_rout_in = sem("w_rout_in")
        w_exp_in = sem("w_exp_in")
        bias_made = sem("bias_made")
        x_in = [sem(f"x_in{u}") for u in range(U1)]
        x_out = [sem(f"x_out{u}") for u in range(U1)]
        st1_done = sem("st1_done")
        mv1_done = sem("mv1_done")
        sd1_done = sem("sd1_done")
        rs1_done = sem("rs1_done")
        ms1_done = sem("ms1_done")
        nb1_done = sem("nb1_done")
        xn1_act = sem("xn1_act")
        xn1_dve = sem("xn1_dve")
        tr1_done = sem("tr1_done")
        xT1_done = sem("xT1_done")
        xTa_done = sem("xTa_done")
        lgT_psum = sem("lgT_psum")
        lgT_done = sem("lgT_done")
        lg_psum = sem("lg_psum")
        lg_done = sem("lg_done")
        rt_step = sem("rt_step")
        oh_done = sem("oh_done")
        dsp = sem("dsp")
        tot_ready = sem("tot_ready")
        tot_psum = sem("tot_psum")
        te_ready = sem("te_ready")
        te_psum = sem("te_psum")
        te_done = sem("te_done")
        tok_split = sem("tok_split")
        slot_oh = sem("slot_oh")
        tile_oh = sem("tile_oh")
        tok_done = sem("tok_done")
        list_mm = sem("list_mm")
        idx_done = sem("idx_done")
        gcol_set = sem("gcol_set")
        scol_set = sem("scol_set")
        gathered = [sem(f"gathered{s}") for s in range(SLOTS)]
        scattered = [sem(f"scattered{s}") for s in range(SLOTS)]
        xn2_done = sem("xn2_done")
        tr2_done = sem("tr2_done")
        xT2_done = sem("xT2_done")
        h_psum = sem("h_psum")
        w_now_in = [sem(f"w_now_in{s}") for s in range(SLOTS)]
        hT_done = sem("hT_done")
        y_psum = sem("y_psum")
        y_done = sem("y_done")
        ones_set = sem("ones_set")
        xa_in = sem("xa_in")
        v_psum = sem("v_psum")
        v_done = sem("v_done")
        q_psum = sem("q_psum")
        k_psum = sem("k_psum")
        q_done = sem("q_done")
        k_done = sem("k_done")
        s_psum = sem("s_psum")
        max_done = sem("max_done")
        exp_done = sem("exp_done")
        pt_psum = sem("pt_psum")
        pt_even = sem("pt_even")
        pt_odd = sem("pt_odd")
        o_psum = sem("o_psum")
        oraw_done = sem("oraw_done")
        ob_psum = sem("ob_psum")
        rs_done = sem("rs_done")
        on_done = sem("on_done")
        oT_psum = sem("oT_psum")
        oT_done = sem("oT_done")
        r_psum = sem("r_psum")
        att_done = sem("att_done")
        added = sem("added")

        block = ctx.enter_context(nc.Block())

        @block.sync
        def _(sp):
            def load_x(k, u):
                seg = x_seg[k] if isinstance(k, int) else x_seg[bass.ds(k, 1)].rearrange("a p n -> (a p) n")
                sp.dma_start(xin[:, u, :, 0:D], seg.rearrange("p (r c) -> p r c", r=R)).then_inc(x_in[u], 16)

            load_x(0, 0)
            load_x(1, 1)
            sp.dma_start(r_w_s[:, :, :], r_w).then_inc(w_rout_in, 16)
            sp.dma_start(r_b_s[:, :], r_b.rearrange("(e a) -> e a", a=1)).then_inc(w_rout_in, 16)
            for u in range(2, U1):
                load_x(u, u)
            sp.dma_start(heads8[:, :], consts).then_inc(const_in, 16)
            sp.dma_start(b_qk_s[:, :], b_qk).then_inc(const_in, 16)
            sp.dma_start(w_in_s[:, :, :], w_in).then_inc(w_attn_in, 16)
            sp.dma_start(w_out_s[:, :, :], w_out).then_inc(w_attn_in, 16)
            sp.dma_start(b_v_s[:, :], b_v.rearrange("(a n) -> a n", a=1).broadcast_to([P, D])).then_inc(w_attn_in, 16)
            sp.dma_start(b_out_s[:, :], b_out.rearrange("(a n) -> a n", a=1).broadcast_to([P, D])).then_inc(w_attn_in, 16)

            def router_steps(i, later, more):
                for u in range(U1):
                    k = i * U1 + u
                    sp.wait_ge(rs1_done, k + 1)
                    seg = rows_seg[k] if isinstance(k, int) else rows_seg[bass.ds(k, 1)].rearrange("a p n -> (a p) n")
                    sp.dma_start(seg, xin[:, u, :, :].rearrange("p r c -> p (r c)")).then_inc(x_out[u], 16)
                    if (later or u) and (more or not u):
                        b = (u - 1) % U1
                        sp.wait_ge(x_out[b], (i + (u > 0)) * 16)
                        sp.wait_ge(xn1_act, k)
                        sp.wait_ge(xn1_dve, k)
                        load_x(k + U1 - 1, b)

            router_steps(0, False, True)
            with sp.Fori(1, NSEG // U1 - 1) as i:
                router_steps(i, True, True)
            router_steps(NSEG // U1 - 1, True, False)
            sp.dma_start(w1_s[:, :, :], w1).then_inc(w_exp_in, 16)
            sp.dma_start(w2_s[:, :, :], w2).then_inc(w_exp_in, 16)

            def segment_in(i, later):
                if later:
                    sp.wait_ge(v_psum, i)
                    sp.wait_ge(q_psum, i)
                    sp.wait_ge(k_psum, i)
                sp.dma_start(xa[:, :, :].rearrange("p c n -> p (c n)"),
                             xTa[:, bass.ds(i, 1), :, :].rearrange("p a c n -> p (a c n)")).then_inc(xa_in, 16)

            def expert_in(s, n, experts, later):
                if later:
                    sp.wait_ge(y_psum, n - SLOTS + 1)
                for t in range(2):
                    sp.dma_start(w1_now[:, s, t, :],
                                 w1_s[:, bass.ds(experts[t], 1), :].rearrange("p a n -> p (a n)"))\
                        .then_inc(w_now_in[s], 16)
                    sp.dma_start(w2_now[:, s, t, :],
                                 w2_s[:, bass.ds(experts[t], 1), :].rearrange("p a n -> p (a n)"))\
                        .then_inc(w_now_in[s], 16)

            sp.wait_ge(xTa_done, NSEG)
            sp.wait_ge(te_done, 1)
            sp.wait_ge(w_exp_in, 32)

            def loop_step(i, later):
                experts = [sp.value_load(te_i[0:1, bass.ds(i * 2 * SLOTS + m, 1)], min_val=0, max_val=E - 1)
                           for m in range(2 * SLOTS)]
                for s in range(SLOTS):
                    expert_in(s, i * SLOTS + s, experts[2 * s:2 * s + 2], later)
                    if s == 0:
                        segment_in(i, later)

            loop_step(0, False)
            with sp.Fori(1, NSEG) as i:
                loop_step(i, True)

        @block.gpsimd
        def _(pool):
            done = [0]

            def step(ins):
                done[0] += 1
                ins.then_inc(pool_set, 1)

            step(pool.memset(eps[:, :], EPS))
            step(pool.memset(power[:, :], -0.5))
            step(pool.memset(zero4[:, :], 0.0))
            step(pool.memset(ident[:, :], 0.0))
            pool.wait_ge(pool_set, 4)
            step(pool.affine_select(out=ident[:, :], in_=ident[:, :], compare_op=ALU.not_equal, fill=1.0,
                                    base=0, pattern=[[-1, P]], channel_multiplier=1))
            step(pool.iota(rank_i[:, :], [[-1, E]], base=E, channel_multiplier=0))
            pool.wait_ge(pool_set, 6)
            step(pool.tensor_copy(rank[:, :], rank_i[:, :]))

            def others():
                step(pool.memset(causal[:, :], 0.0))
                step(pool.memset(before[:, :], 1.0))
                step(pool.memset(onesb[:, :], 1.0))
                step(pool.memset(zeros[:, :], 0.0))
                step(pool.iota(iota_i[:, :], [[1, P]], base=0, channel_multiplier=0))
                step(pool.iota(part_i[:, :], [[0, 1]], base=0, channel_multiplier=1))
                step(pool.iota(tok_i[:, :].rearrange("p (s r) -> p s r", r=R), [[P * R, NSEG], [1, R]], base=1,
                               channel_multiplier=R))
                step(pool.memset(gidx[:, NTILE:NIDX], 0.0))
                step(pool.memset(ends[:, 0:1], 0.0))
                step(pool.memset(v[:, :, DH + 1:HS], 0.0))
                step(pool.memset(v[:, :, DH:DH + 1], 1.0))
                pool.wait_ge(pool_set, done[0])
                step(pool.tensor_copy(identb[:, :], ident[:, :]))
                step(pool.affine_select(out=causal[:, :], in_=causal[:, :], compare_op=ALU.is_ge, fill=NEG,
                                        base=0, pattern=[[-1, P]], channel_multiplier=1))
                step(pool.affine_select(out=before[:, :], in_=before[:, :], compare_op=ALU.is_gt, fill=0.0,
                                        base=0, pattern=[[1, P]], channel_multiplier=-1))
                step(pool.tensor_copy(iota[:, :], iota_i[:, :]))
                step(pool.tensor_copy(part[:, :], part_i[:, :]))
            others()
            assert done[0] == SETUP
            def keep(k, u):
                pool.wait_ge(xT1_done, k + 1)
                pool.tensor_copy(xTa[:, bass.ds(k, 1), :, :].rearrange("p a c n -> p (a c) n"),
                                 xT1[:, u % 2, :, 0, :]).then_inc(xTa_done, 1)

            def router_steps(i, later):
                for u in range(U1):
                    k = i * U1 + u
                    pool.wait_ge(mv1_done, k + 1)
                    pool.tensor_tensor(sd1[:, :], xin[:, u, :, D + 1], eps[:, :], ALU.add).then_inc(sd1_done, 1)
                    pool.wait_ge(sd1_done, k + 1)
                    pool.tensor_tensor(xin[:, u, :, D + 1], sd1[:, :], power[:, :], ALU.pow).then_inc(rs1_done, 1)
                    pool.wait_ge(rs1_done, k + 1)
                    pool.tensor_tensor(ms1[:, :], xin[:, u, :, D], xin[:, u, :, D + 1], ALU.mult).then_inc(ms1_done, 1)
                    pool.wait_ge(ms1_done, k + 1)
                    pool.tensor_tensor(nb1[:, u, :], zero4[:, :], ms1[:, :], ALU.subtract).then_inc(nb1_done, 1)
                    if later or u >= 2:
                        keep(k - 2, u)

            router_steps(0, False)
            with pool.Fori(1, NSEG // U1) as i:
                router_steps(i, True)
            keep(NSEG - 2, 0)
            keep(NSEG - 1, 1)
            pool.wait_ge(tok_split, 3)

            def list_steps(i, later):
                for u in range(2):
                    n = i * 2 + u
                    pool.wait_ge(tile_oh, n + 1)
                    if later:
                        pool.wait_ge(list_mm, n - 1)
                    pool.tensor_tensor(tok_at[:, u, :, :, :],
                                       at_tile[:, u, :, None, :].broadcast_to([P, 4, 2, NTILE]),
                                       tok_parts[:, bass.ds(n * 4, 4), :][:, :, :, None]
                                       .broadcast_to([P, 4, 2, NTILE]), ALU.mult).then_inc(tok_done, 1)

            list_steps(0, False)
            with pool.Fori(1, T // 8) as i:
                list_steps(i, True)

            def gather(s, n):
                for t in range(2):
                    pool.indirect_dma_start(out=xg[:, s, t, :], out_offset=None, in_=rows[:, :],
                                            in_offset=bass.IndirectOffsetOnAxis(ap=gcol[:, s, t:t + 1], axis=0))\
                        .then_inc(gathered[s], 16)

            pool.wait_ge(idx_done, 1)
            for s in range(SLOTS):
                pool.tensor_copy(gcol[:, s, :], gidx[:, 2 * s:2 * s + 2]).then_inc(gcol_set, 1)
            pool.wait_ge(gcol_set, SLOTS)
            for u in range(U1):
                pool.wait_ge(x_out[u], 16 * (NSEG // U1))
            for s in range(SLOTS):
                gather(s, s)
            def loop_step(i, later):
                for s in range(SLOTS):
                    n = i * SLOTS + s
                    if later:
                        pool.wait_ge(scattered[s], i * 32)
                    pool.tensor_copy(scol[:, s, :], sidx[:, bass.ds(n * 2, 2)]).then_inc(scol_set, 1)
                    pool.wait_ge(gathered[s], i * 32 + 32)
                    pool.tensor_copy(gcol[:, s, :], gidx[:, bass.ds(n * 2 + 2 * SLOTS, 2)]).then_inc(gcol_set, 1)
                    pool.wait_ge(scol_set, n + 1)
                    pool.wait_ge(gcol_set, n + 1 + SLOTS)
                    pool.wait_ge(y_done, n + 1)
                    pool.sem_inc(passed_pool, 1)
                    for t in range(2):
                        pool.indirect_dma_start(out=out_rows[:, :],
                                                out_offset=bass.IndirectOffsetOnAxis(ap=scol[:, s, t:t + 1], axis=0),
                                                in_=yb[:, s, t, :], in_offset=None, bounds_check=NTOK - 1,
                                                oob_is_err=False).then_inc(scattered[s], 16)
                    gather(s, n)

            loop_step(0, False)
            with pool.Fori(1, NSEG) as i:
                loop_step(i, True)
            for s in range(SLOTS):
                pool.wait_ge(scattered[s], 32 * NSEG)
                pool.wait_ge(gathered[s], 32 * NSEG + 32)
            pool.wait_ge(att_done, NSEG)
            pool.dma_start(att_rows, att[:, :, :], accum_op=ALU.add).then_inc(added, 16)
            pool.wait_ge(added, 16)

        @block.vector
        def _(dve):
            dve.wait_ge(pool_set, 7)

            def normalise_last(k, u):
                dve.wait_ge(rs1_done, k + 1)
                dve.tensor_scalar(xn1[:, u % 2, R - 1, :], xin[:, u, R - 1, 0:D], xin[:, u, R - 1, D:D + 1],
                                  xin[:, u, R - 1, D + 1:D + 2], ALU.subtract, ALU.mult).then_inc(xn1_dve, 1)

            def choose(i):
                dve.wait_ge(lg_psum, i * U1)
                dve.tensor_copy(lg[:, :, :].rearrange("p r e -> p (r e)"), bank[5][:, :]).then_inc(lg_done, 1)
                dve.wait_ge(lg_done, i)
                dve.reduce_max(lmax[:, :], lg[:, :, :], AX.X).then_inc(rt_step, 1)
                dve.wait_ge(rt_step, i * 4 - 3)
                n = U1 * R
                dve.tensor_tensor(hit[:, :, :], lg[:, :, :], lmax[:, :, None].broadcast_to([P, n, E]),
                                  ALU.is_equal).then_inc(rt_step, 1)
                dve.wait_ge(rt_step, i * 4 - 2)
                dve.tensor_tensor(hit[:, :, :], hit[:, :, :], rank[:, None, :].broadcast_to([P, n, E]),
                                  ALU.mult).then_inc(rt_step, 1)
                dve.wait_ge(rt_step, i * 4 - 1)
                dve.reduce_max(first[:, :], hit[:, :, :], AX.X).then_inc(rt_step, 1)
                dve.wait_ge(rt_step, i * 4)
                dve.tensor_tensor(onehot[:, :, bass.ds(i * n - n, n)].rearrange("p e r -> p r e"),
                                  rank[:, None, :].broadcast_to([P, n, E]),
                                  first[:, :, None].broadcast_to([P, n, E]), ALU.is_equal).then_inc(oh_done, 1)

            def router_steps(i, later):
                for u in range(U1):
                    k = i * U1 + u
                    if later or u >= 2:
                        dve.wait_ge(mv1_done, k - 1)
                    dve.wait_ge(x_in[u], i * 16 + 16)
                    for r in range(R):
                        last = dve.bn_stats(st1[:, u % 2, r, :], xin[:, u, r, 0:D])
                    last.then_inc(st1_done, 1)
                    if later or u:
                        if later or u >= 3:
                            dve.wait_ge(tr1_done, k - 2)
                        normalise_last(k - 1, (u - 1) % U1)
                    dve.wait_ge(st1_done, k + 1)
                    dve.sem_inc(passed_dve, 1)
                    for r in range(R):
                        last = dve.bn_aggr(xin[:, u, r, D:D + 2], st1[:, u % 2, r, :])
                    last.then_inc(mv1_done, 1)
                    if later and u == U1 - 1:
                        choose(i)

            router_steps(0, False)
            with dve.Fori(1, NSEG // U1) as i:
                router_steps(i, True)
            dve.wait_ge(tr1_done, NSEG - 2)
            normalise_last(NSEG - 1, U1 - 1)
            choose(NSEG // U1)
            steps = [0]

            def step(ins):
                steps[0] += 1
                ins.then_inc(dsp, 1)
                dve.wait_ge(dsp, steps[0])

            dve.wait_ge(pool_set, SETUP)
            dve.wait_ge(oh_done, NSEG // U1)
            oh_flat = onehot[:, :, :].rearrange("p e t -> p (e t)")
            dve.tensor_scalar(tok_hi[:, :], tok_i[:, :], 6, None, ALU.arith_shift_right).then_inc(tok_split, 1)
            dve.tensor_scalar(tok_lo[:, :], tok_i[:, :], 63, None, ALU.bitwise_and).then_inc(tok_split, 1)
            step(dve.tensor_tensor_scan(count[:, :, :].rearrange("p e t -> p (e t)"), oh_flat, oh_flat, 0.0,
                                        ALU.add, ALU.max))
            step(dve.tensor_copy(ends[:, 1:E + 1], count[:, :, T - 1]))
            dve.wait_ge(tok_split, 2)
            dve.tensor_copy(tok_parts[:, :, 0], tok_hi[:, :])
            dve.tensor_copy(tok_parts[:, :, 1], tok_lo[:, :]).then_inc(tok_split, 1)
            dve.tensor_tensor(rowtot[:, :], ends[:, 1:E + 1], ends[:, 0:E], ALU.subtract).then_inc(tot_ready, 1)
            dve.wait_ge(tot_psum, 1)
            step(dve.tensor_scalar(cnt_i[:, :], bank[0][:, E:2 * E], float(P - 1), None, ALU.add))
            step(dve.tensor_scalar(til_i[:, :], cnt_i[:, :], 7, None, ALU.arith_shift_right))
            step(dve.tensor_copy(til[:, :], til_i[:, :]))
            step(dve.tensor_tensor_scan(cum[:, :], til[:, :], til[:, :], 0.0, ALU.add, ALU.max))
            step(dve.tensor_scalar(past[:, :], cum[:, :], part[:, 0:1], None, ALU.is_le))
            step(dve.reduce_sum(te0[:, :], past[:, :], AX.X))
            dve.tensor_scalar(te1[:, :], te0[:, :], float(E - 1), None, ALU.min).then_inc(te_ready, 1)
            step(dve.tensor_tensor(offs[:, :], cum[:, :], til[:, :], ALU.subtract))
            step(dve.scalar_tensor_tensor(base0[:, :], offs[:, :], float(P), bank[0][:, 0:E], ALU.mult, ALU.add))
            step(dve.scalar_tensor_tensor(base[:, :], base0[:, :], -1.0, ends[:, 0:E], ALU.add, ALU.subtract))
            step(dve.tensor_tensor(place[:, :, :], count[:, :, :], base[:, :, None].broadcast_to([P, E, T]), ALU.add))
            step(dve.tensor_tensor(place[:, :, :], place[:, :, :], onehot[:, :, :], ALU.mult))
            step(dve.reduce_sum(pos[:, :], place[:, :, :].rearrange("p e t -> p t e"), AX.X))
            step(dve.tensor_copy(pos_i[:, :], pos[:, :]))
            dve.tensor_scalar(slot_i[:, :], pos_i[:, :], P - 1, None, ALU.bitwise_and)
            step(dve.tensor_scalar(tile_i[:, :], pos_i[:, :], 7, None, ALU.arith_shift_right))
            step(dve.tensor_copy(slot_b[:, :], slot_i[:, :]))
            step(dve.tensor_copy(tile_b[:, :], tile_i[:, :]))
            dve.wait_ge(te_psum, 1)
            dve.tensor_copy(te_i[0:1, :], bank[1][0:1, 0:P]).then_inc(te_done, 1)
            def list_steps(i, later):
                for u in range(2):
                    n = i * 2 + u
                    if later:
                        dve.wait_ge(list_mm, n - 1)
                    dve.tensor_tensor(at_tile[:, u, :, :], iota[:, None, 0:NTILE].broadcast_to([P, 4, NTILE]),
                                      tile_b[:, bass.ds(n * 4, 4)][:, :, None].broadcast_to([P, 4, NTILE]),
                                      ALU.is_equal).then_inc(tile_oh, 1)
                    dve.tensor_tensor(at_slot[:, u, :, :], iota[:, None, :].broadcast_to([P, 4, P]),
                                      slot_b[:, bass.ds(n * 4, 4)][:, :, None].broadcast_to([P, 4, P]),
                                      ALU.is_equal).then_inc(slot_oh, 1)

            list_steps(0, False)
            with dve.Fori(1, T // 8) as i:
                list_steps(i, True)
            dve.wait_ge(list_mm, T // 4 + 1)
            step(dve.tensor_copy(listed[:, :], bank[2][:, NTILE:2 * NTILE]))
            step(dve.scalar_tensor_tensor(listed[:, :], bank[2][:, 0:NTILE], 64.0, listed[:, :], ALU.mult, ALU.add))
            dve.tensor_scalar(gidx[:, 0:NTILE], listed[:, :], -1.0, 0.0, ALU.add, ALU.max)
            step(dve.tensor_scalar(empty[:, :], listed[:, :], 0.0, FAR, ALU.is_equal, ALU.mult))
            dve.scalar_tensor_tensor(sidx[:, :], listed[:, :], -1.0, empty[:, :], ALU.add, ALU.add)\
                .then_inc(idx_done, 1)
            dve.memset(hT[HID:HID + 1, :, :], 1.0).then_inc(ones_set, 1)

            def normalise(s, n, turn):
                dve.wait_ge(gathered[s], turn * 32 + 32)
                for t in range(2):
                    last = dve.tensor_scalar(xn2[:, s, t, :], xg[:, s, t, 0:D], xg[:, s, t, D:D + 1],
                                             xg[:, s, t, D + 1:D + 2], ALU.subtract, ALU.mult)
                last.then_inc(xn2_done, 1)

            def sums(s, n, i, later):
                dve.wait_ge(y_psum, n + 1)
                if later:
                    dve.wait_ge(scattered[s], i * 32)
                dve.scalar_tensor_tensor(yb[:, s, :, :], b_y[:, :].rearrange("p (t c) -> p t c", t=2), 0.0,
                                         xg[:, s, :, 0:D], ALU.max, ALU.add).then_inc(y_done, 1)

            def turn_probs(j, i):
                dve.wait_ge(pt_psum, i * BANKS + j + 1)
                dve.tensor_copy(probsT[:, 4 * j:4 * j + 4, :].rearrange("p n k -> p (n k)"), bank[j][:, :])\
                    .then_inc(pt_even, 1)

            def norm_out(i):
                dve.wait_ge(ob_psum, i)
                o = b_o[:, :].rearrange("p (h d) -> p h d", h=NH)
                dve.reciprocal(rsum[:, :], o[:, :, DH]).then_inc(rs_done, 1)
                dve.wait_ge(rs_done, i)
                dve.tensor_tensor(on[:, :, :], o[:, :, 0:DH], rsum[:, :, None].broadcast_to([P, NH, DH]), ALU.mult)\
                    .then_inc(on_done, 1)

            def bias_out(i):
                dve.wait_ge(r_psum, i)
                dve.tensor_tensor(att[:, bass.ds(i - 1, 1), :].rearrange("p a c -> p (a c)"), b_v_k[:, 0:D],
                                  b_out_s[:, :], ALU.add).then_inc(att_done, 1)

            def values(i):
                dve.wait_ge(v_psum, i + 1)
                dve.tensor_tensor(v[:, :, 0:DH], b_v_k[:, 0:D].rearrange("p (h d) -> p h d", h=NH),
                                  b_v_s[:, :].rearrange("p (h d) -> p h d", h=NH), ALU.add).then_inc(v_done, 1)

            def keys(i):
                dve.wait_ge(k_psum, i + 1)
                for g in range(C):
                    dve.scalar_tensor_tensor(
                        kT[:, g, :, :], b_v_k[:, g * P:(g + 1) * P][:, None, :].broadcast_to([P, 8, P]),
                        b_qk_s[:, C + g:C + g + 1], heads8[:, :, None].broadcast_to([P, 8, P]), ALU.add, ALU.mult)\
                        .then_inc(k_done, 1)

            def maxima(j, i):
                dve.wait_ge(s_psum, i * BANKS + j + 1)
                dve.tensor_reduce(nmax[:, 4 * j:4 * j + 4], bank[j][:, :].rearrange("p (n k) -> p n k", n=4),
                                  AX.X, ALU.max, negate=True).then_inc(max_done, 1)

            normalise(0, 0, 0)
            dve.wait_ge(w_attn_in, 64)
            dve.wait_ge(const_in, 32)

            def loop_step(i, later):
                n = i * SLOTS
                normalise(1, n + 1, i)
                if later:
                    norm_out(i)
                values(i)
                sums(0, n, i, later)
                keys(i)
                normalise(2, n + 2, i)
                sums(1, n + 1, i, later)
                maxima(0, i)
                maxima(1, i)
                if later:
                    bias_out(i)
                maxima(2, i)
                maxima(3, i)
                normalise(0, n + 3, i + 1)
                turn_probs(0, i)
                turn_probs(2, i)
                sums(2, n + 2, i, later)

            loop_step(0, False)
            with dve.Fori(1, NSEG) as i:
                loop_step(i, True)
            norm_out(NSEG)
            bias_out(NSEG)

        @block.scalar
        def _(act):
            def turn_x1(k, u):
                act.wait_ge(tr1_done, k + 1)
                if not isinstance(k, int) or k >= 2:
                    act.wait_ge(xTa_done, k - 1)
                for c in range(C):
                    last = act.activation(xT1[:, u % 2, c, :, :].rearrange("p r n -> p (r n)"),
                                          bank[2 * (u % 2) + c][:, :], ACT.Copy)
                last.then_inc(xT1_done, 1)

            def logits_out(k, u):
                act.wait_ge(lgT_psum, k + 1)
                act.activation(lgT[:, u % 2, :], bank[4][0:E, :], ACT.Identity, bias=r_b_s[:, 0:1])\
                    .then_inc(lgT_done, 1)

            act.wait_ge(pool_set, 1)
            act.activation(warm[:, :], eps[:, :], ACT.Identity)
            act.wait_ge(w_rout_in, 32)

            def router_steps(i, later):
                for u in range(U1):
                    k = i * U1 + u
                    if later or u:
                        if later or u >= 3:
                            turn_x1(k - 1, (u - 1) % U1)
                        else:
                            turn_x1(u - 1, u - 1)
                    act.wait_ge(nb1_done, k + 1)
                    if later or u >= 2:
                        act.wait_ge(tr1_done, k - 1)
                    for r in range(R - 1):
                        last = act.activation(xn1[:, u % 2, r, :], xin[:, u, r, 0:D], ACT.Identity,
                                              scale=xin[:, u, r, D + 1:D + 2], bias=nb1[:, u, r:r + 1])
                    last.then_inc(xn1_act, 1)
                    if later or u >= 2:
                        logits_out(k - 2, (u - 2) % U1)

            router_steps(0, False)
            with act.Fori(1, NSEG // U1) as i:
                router_steps(i, True)
            turn_x1(NSEG - 1, U1 - 1)
            logits_out(NSEG - 2, U1 - 2)
            logits_out(NSEG - 1, U1 - 1)
            act.wait_ge(const_in, 32)
            act.activation(q_bias[:, :], b_qk_s[:, 0:C], ACT.Copy, scale=DH ** -0.5).then_inc(bias_made, 1)

            def turn_probs(j, i):
                act.wait_ge(pt_psum, i * BANKS + j + 1)
                act.activation(probsT[:, 4 * j:4 * j + 4, :].rearrange("p n k -> p (n k)"), bank[j][:, :], ACT.Copy)\
                    .then_inc(pt_odd, 1)

            def turn_x(n):
                act.wait_ge(tr2_done, n + 1)
                act.activation(xT2[:, :, :, :].rearrange("p c t n -> p (c t n)"), b_x[:, :], ACT.Copy)\
                    .then_inc(xT2_done, 1)

            def hidden(s, n):
                act.wait_ge(h_psum, n + 1)
                for t in range(2):
                    last = act.activation(hT[0:HID, t, :], b_x[0:HID, t * P:(t + 1) * P], ACT.Relu,
                                          bias=w2_now[0:HID, s, t, D:D + 1])
                last.then_inc(hT_done, 1)

            def raw_out(i):
                act.wait_ge(o_psum, i)
                act.activation(oraw[:, :], b_o[:, :], ACT.Copy).then_inc(oraw_done, 1)

            def queries(i):
                act.wait_ge(q_psum, i + 1)
                for c in range(C):
                    last = act.activation(qT[:, c, :], b_o[:, c * P:(c + 1) * P], ACT.Identity, scale=DH ** -0.5,
                                          bias=q_bias[:, c:c + 1])
                last.then_inc(q_done, 1)

            def turn_out(i):
                act.wait_ge(oT_psum, i)
                act.activation(oT[:, :, :].rearrange("p c n -> p (c n)"), b_v_k[:, 0:D], ACT.Copy).then_inc(oT_done, 1)

            def exps(j, i):
                act.wait_ge(max_done, i * BANKS + j + 1)
                for m in range(4):
                    last = act.activation(probs[:, 4 * j + m, :], bank[j][:, m * P:(m + 1) * P], ACT.Exp,
                                          bias=nmax[:, 4 * j + m:4 * j + m + 1])
                last.then_inc(exp_done, 1)

            act.wait_ge(bias_made, 1)

            def loop_step(i, later):
                n = i * SLOTS
                turn_x(n)
                if later:
                    raw_out(i)
                hidden(0, n)
                turn_x(n + 1)
                hidden(1, n + 1)
                queries(i)
                if later:
                    turn_out(i)
                exps(0, i)
                exps(1, i)
                exps(2, i)
                turn_x(n + 2)
                exps(3, i)
                hidden(2, n + 2)
                turn_probs(1, i)
                turn_probs(3, i)

            loop_step(0, False)
            with act.Fori(1, NSEG) as i:
                loop_step(i, True)
            raw_out(NSEG)
            turn_out(NSEG)

        @block.tensor
        def _(pe):
            pe.wait_ge(pool_set, 7)
            pe.wait_ge(w_rout_in, 32)
            def transposed(k, u):
                pe.wait_ge(xn1_act, k + 1)
                pe.wait_ge(xn1_dve, k + 1)
                for c in range(C):
                    for r in range(R):
                        last = pe.transpose(bank[2 * (u % 2) + c][:, r * P:(r + 1) * P],
                                            xn1[:, u % 2, r, c * P:(c + 1) * P], ident[:, :])
                last.then_inc(tr1_done, 1)

            def logits(k, u, after):
                pe.wait_ge(xT1_done, k + 1)
                if after:
                    pe.wait_ge(lgT_done, k)
                for c in range(C):
                    last = pe.matmul(bank[4][0:E, :], r_w_s[:, c, :],
                                     xT1[:, u % 2, c, :, :].rearrange("p r n -> p (r n)"),
                                     start=(c == 0), stop=(c == C - 1))
                last.then_inc(lgT_psum, 1)

            def logits_back(k, u, i, copied):
                pe.wait_ge(lgT_done, k + 1)
                if copied:
                    pe.wait_ge(lg_done, i)
                pe.sem_inc(passed_pe, 1)
                for r in range(R):
                    last = pe.transpose(bank[5][:, (u * R + r) * E:(u * R + r + 1) * E],
                                        lgT[:, u % 2, r * P:(r + 1) * P], ident[0:E, 0:E])
                last.then_inc(lg_psum, 1)

            def router_steps(i, later):
                for u in range(U1):
                    k = i * U1 + u
                    transposed(k, u)
                    if later or u:
                        logits(k - 1, (u - 1) % U1, later or u >= 2)
                    if later or u >= 2:
                        logits_back(k - 2, (u - 2) % U1, i, later and u == 2)

            router_steps(0, False)
            with pe.Fori(1, NSEG // U1) as i:
                router_steps(i, True)
            logits(NSEG - 1, U1 - 1, True)
            logits_back(NSEG - 2, U1 - 2, 0, False)
            logits_back(NSEG - 1, U1 - 1, 0, False)
            pe.wait_ge(tot_ready, 1)
            pe.wait_ge(pool_set, SETUP)
            pe.matmul(bank[0][:, 0:E], before[:, :], rowtot[:, :], start=True, stop=True)
            pe.matmul(bank[0][:, E:2 * E], onesb[:, :], rowtot[:, :], start=True, stop=True).then_inc(tot_psum, 1)
            pe.wait_ge(te_ready, 1)
            pe.matmul(bank[1][0:1, 0:P], te1[:, 0:1], ident[:, :], start=True, stop=True).then_inc(te_psum, 1)
            pe.matmul(bank[2][:, 0:2 * NTILE], onesb[:, :], zeros[:, :], start=True, stop=False)
            def list_steps(i, later):
                for u in range(2):
                    n = i * 2 + u
                    pe.wait_ge(slot_oh, n + 1)
                    pe.wait_ge(tok_done, n + 1)
                    for m in range(4):
                        last = pe.matmul(bank[2][:, 0:2 * NTILE], at_slot[:, u, m, :],
                                         tok_at[:, u, m, :, :].rearrange("p a n -> p (a n)"),
                                         start=False, stop=False)
                    last.then_inc(list_mm, 1)

            list_steps(0, False)
            with pe.Fori(1, T // 8) as i:
                list_steps(i, True)
            pe.matmul(bank[2][:, 0:2 * NTILE], onesb[:, :], zeros[:, :], start=False, stop=True).then_inc(list_mm, 1)

            def turn_x(s, n, later):
                pe.wait_ge(xn2_done, n + 1)
                if later:
                    pe.wait_ge(hT_done, n)
                for c in range(C):
                    for t in range(2):
                        last = pe.transpose(b_x[:, (2 * c + t) * P:(2 * c + t + 1) * P],
                                            xn2[:, s, t, c * P:(c + 1) * P], ident[:, :])
                last.then_inc(tr2_done, 1)

            def hidden(s, n, i):
                pe.wait_ge(xT2_done, n + 1)
                pe.wait_ge(w_now_in[s], i * 64 + 64)
                for t in range(2):
                    for c in range(C):
                        last = pe.matmul(b_x[0:HID, t * P:(t + 1) * P], w1_now[:, s, t, c * HID:(c + 1) * HID],
                                         xT2[:, c, t, :], start=(c == 0), stop=(c == C - 1))
                last.then_inc(h_psum, 1)

            def outputs(s, n, later):
                pe.wait_ge(hT_done, n + 1)
                if later:
                    pe.wait_ge(y_done, n)
                for t in range(2):
                    last = pe.matmul(b_y[:, t * D:(t + 1) * D], hT[:, t, :], w2_now[:, s, t, 0:D],
                                     start=True, stop=True)
                last.then_inc(y_psum, 1)

            def attend(i):
                pe.wait_ge(pt_even, i * 2)
                pe.wait_ge(pt_odd, i * 2)
                pe.wait_ge(v_done, i)
                pe.wait_ge(q_done, i)
                for h in range(NH):
                    rows_h = slice(HS * (h % 4), HS * (h % 4 + 1))
                    last = pe.matmul(b_o[rows_h, h // 4 * P:(h // 4 + 1) * P], v[:, h, :], probsT[:, h, :],
                                     start=True, stop=True)
                last.then_inc(o_psum, 1)

            def back(i):
                pe.wait_ge(oraw_done, i)
                for g in range(4):
                    last = pe.transpose(b_o[:, g * P:(g + 1) * P], oraw[:, g * P:(g + 1) * P], ident[:, :])
                last.then_inc(ob_psum, 1)

            def turn_out(i):
                pe.wait_ge(on_done, i)
                if not isinstance(i, int) or i < NSEG:
                    pe.wait_ge(k_done, i * C + C)
                flat = on[:, :, :].rearrange("p h d -> p (h d)")
                for c in range(C):
                    last = pe.transpose(b_v_k[:, c * P:(c + 1) * P], flat[:, c * P:(c + 1) * P], ident[:, :])
                last.then_inc(oT_psum, 1)

            def project(i):
                pe.wait_ge(oT_done, i)
                for c in range(C):
                    last = pe.matmul(b_v_k[:, 0:D], oT[:, c, :], w_out_s[:, c, :], start=(c == 0), stop=(c == C - 1))
                last.then_inc(r_psum, 1)

            def values(i, later):
                pe.wait_ge(xa_in, i * 16 + 16)
                if later:
                    pe.wait_ge(k_done, i * C)
                for c in range(C):
                    last = pe.matmul(b_v_k[:, 0:D], xa[:, c, :], w_in_s[:, c, 2 * D:3 * D], start=(c == 0),
                                     stop=(c == C - 1))
                last.then_inc(v_psum, 1)

            def projected(to, first, count_up):
                for g in range(C):
                    for c in range(C):
                        last = pe.matmul(to[:, g * P:(g + 1) * P], w_in_s[:, c, first + g * P:first + (g + 1) * P],
                                         xa[:, c, :], start=(c == 0), stop=(c == C - 1))
                last.then_inc(count_up, 1)

            def keys(i):
                pe.wait_ge(v_done, i + 1)
                projected(b_v_k, D, k_psum)

            def queries(i, later):
                if later:
                    pe.wait_ge(on_done, i)
                projected(b_o, 0, q_psum)

            def scores(j, i, later):
                pe.wait_ge(q_done, i + 1)
                pe.wait_ge(k_done, i * C + 1 + j // 2)
                if later:
                    pe.wait_ge(pt_even, i * 2)
                    pe.wait_ge(pt_odd, i * 2)
                pe.matmul(bank[j][:, :], identb[:, :], causal[:, None, :].broadcast_to([P, 4, P]), start=True,
                          stop=False)
                pe.matmul(bank[j][:, :], qT[:, j // 2, :],
                          kT[:, j // 2, j % 2 * 4:j % 2 * 4 + 4, :].rearrange("p m n -> p (m n)"), start=False,
                          stop=True).then_inc(s_psum, 1)

            def turn_probs(j, i):
                pe.wait_ge(exp_done, i * BANKS + j + 1)
                for m in range(4):
                    last = pe.transpose(bank[j][:, m * P:(m + 1) * P], probs[:, 4 * j + m, :], ident[:, :])
                last.then_inc(pt_psum, 1)

            pe.wait_ge(idx_done, 1)
            pe.wait_ge(ones_set, 1)
            pe.wait_ge(w_attn_in, 64)

            def loop_step(i, later):
                n = i * SLOTS
                turn_x(0, n, later)
                if later:
                    attend(i)
                hidden(0, n, i)
                if later:
                    back(i)
                values(i, later)
                outputs(0, n, later)
                turn_x(1, n + 1, True)
                keys(i)
                hidden(1, n + 1, i)
                queries(i, later)
                outputs(1, n + 1, True)
                scores(0, i, later)
                if later:
                    turn_out(i)
                scores(1, i, later)
                if later:
                    project(i)
                scores(2, i, later)
                scores(3, i, later)
                turn_x(2, n + 2, True)
                turn_probs(0, i)
                turn_probs(1, i)
                hidden(2, n + 2, i)
                turn_probs(2, i)
                turn_probs(3, i)
                outputs(2, n + 2, True)

            loop_step(0, False)
            with pe.Fori(1, NSEG) as i:
                loop_step(i, True)
            attend(NSEG)
            back(NSEG)
            turn_out(NSEG)
            project(NSEG)


def kernel(L0_attn_x, L0_attn_w_in, L0_attn_b_in, L0_attn_w_out, L0_attn_b_out, L0_ffn_router_w, L0_ffn_router_b,
           L0_ffn_weights1, L0_ffn_bias1, L0_ffn_weights2, L0_ffn_bias2):
    import concourse.bacc as bacc
    import numpy as np
    from concourse.bass_utils import run_bass_kernel_spmd

    def rows(a):
        a = np.asarray(a)
        return np.ascontiguousarray(a.reshape(C, P, a.shape[1]).transpose(1, 0, 2))

    b_in = np.asarray(L0_attn_b_in)
    w1 = np.asarray(L0_ffn_weights1).reshape(E, C, P, HID).transpose(2, 0, 1, 3)
    w2 = np.zeros((HID + 1, E, D + 1), np.float32)
    w2[:HID, :, :D] = np.asarray(L0_ffn_weights2).transpose(1, 0, 2)
    w2[HID, :, :D] = np.asarray(L0_ffn_bias2)
    w2[:HID, :, D] = np.asarray(L0_ffn_bias1).T
    consts = np.arange(P)[:, None] // DH == np.arange(8)[None, :]
    arrays = {
        "x": np.asarray(L0_attn_x),
        "consts": consts.astype(np.float32),
        "w_in": rows(np.asarray(L0_attn_w_in).T),
        "b_qk": np.ascontiguousarray(b_in[:2 * D].reshape(2 * C, P).T),
        "b_v": np.ascontiguousarray(b_in[2 * D:]),
        "w_out": rows(np.asarray(L0_attn_w_out).T),
        "b_out": np.asarray(L0_attn_b_out),
        "r_w": rows(np.asarray(L0_ffn_router_w).T),
        "r_b": np.asarray(L0_ffn_router_b),
        "w1": np.ascontiguousarray(w1).reshape(P, E, C * HID),
        "w2": w2,
    }
    nc = bacc.Bacc("TRN2", target_bir_lowering=False, num_devices=1)
    args = [nc.dram_tensor(f"in_{name}", a.shape, mybir.dt.from_np(a.dtype), kind="ExternalInput").ap()
            for name, a in arrays.items()]
    out = nc.dram_tensor("out", arrays["x"].shape, FP32, kind="ExternalOutput").ap()
    build(nc, *args, out)
    r = run_bass_kernel_spmd(nc, [{f"in_{name}": a for name, a in arrays.items()}], core_ids=[0])
    return r.results[0]["out"]
```

```python
from contextlib import ExitStack

import concourse.bass as bass
from concourse import mybir

FP32 = mybir.dt.float32
BF16 = mybir.dt.bfloat16
I32 = mybir.dt.int32
ALU = mybir.AluOpType
ACT = mybir.ActivationFunctionType
AX = mybir.AxisListType

P = 128
D = 256
C = D // P
R = 4
NSEG = 16
NTOK = NSEG * P * R
NH = 16
DH = D // NH
E = 32
HID = D // 4
T = NTOK // P
SLOTS = 3
NPAIR = NSEG * SLOTS
NTILE = 2 * NPAIR
U1 = 4
LIST = 4
BANKS = 4
SETUP = 19
SETUP_ROUTER = 7
MASK = 1e9
HIGH = 3.4028234e38
ROW = D + 2
VS = 3 * DH
FAR = 1048576.0
EPS = 1e-5
assert NTILE >= T + E - 1


def build(nc, x, consts, w_in, b_qk, b_v, w_out, b_out, r_w, r_b, w1, w2, out):
    ctx = ExitStack()
    with ctx:
        def sb(name, shape, dt=FP32):
            return ctx.enter_context(nc.sbuf_tensor(name, shape, dt))

        def sem(name):
            return ctx.enter_context(nc.semaphore(name))

        ident = sb("ident", [P, P])
        causal = sb("causal", [P, P])
        before = sb("before", [P, P], BF16)
        onesb = sb("onesb", [P, P], BF16)
        zeros = sb("zeros", [P, 2 * NTILE], BF16)
        iota_i = sb("iota_i", [P, P], I32)
        iota = sb("iota", [P, P], BF16)
        part_i = sb("part_i", [P, 1], I32)
        part = sb("part", [P, 1])
        rank_i = sb("rank_i", [P, E], I32)
        rank = sb("rank", [P, E])
        heads4 = sb("heads4", [P, 4])
        eps = sb("eps", [P, 4])
        power = sb("power", [P, 4])
        zero4 = sb("zero4", [P, 4])
        warm = sb("warm", [P, 4])
        w_in_s = sb("w_in_s", [P, C, 3 * D])
        b_qk_s = sb("b_qk_s", [P, 2 * C])
        q_bias = sb("q_bias", [P, C])
        b_v_s = sb("b_v_s", [P, D])
        w_out_s = sb("w_out_s", [P, C, D])
        b_out_s = sb("b_out_s", [P, D])
        r_w_s = sb("r_w_s", [P, C, E])
        r_b_s = sb("r_b_s", [P, 1])
        w1_s = sb("w1_s", [P, E, C * HID])
        w2_s = sb("w2_s", [HID + 1, E, D + 1])
        xin = sb("xin", [P, U1, R, ROW])
        st1 = sb("st1", [P, 2, R, 6])
        sd1 = sb("sd1", [P, R])
        ms1 = sb("ms1", [P, R])
        nb1 = sb("nb1", [P, U1, R])
        xn1 = sb("xn1", [P, 2, R, D])
        xT1 = sb("xT1", [P, 2, C, R, P])
        xTa = sb("xTa", [P, NSEG, C, P])
        lgT = sb("lgT", [P, 2, P])
        lg = sb("lg", [P, U1 * R, E])
        lmax = sb("lmax", [P, U1 * R])
        hit = sb("hit", [P, U1 * R, E])
        first = sb("first", [P, U1 * R])
        onehot = sb("onehot", [P, E, T])
        count = sb("count", [P, E, T])
        place = sb("place", [P, E, T])
        ends = sb("ends", [P, E + 1])
        rowtot = sb("rowtot", [P, E], BF16)
        cnt_i = sb("cnt_i", [P, E], I32)
        til_i = sb("til_i", [P, E], I32)
        til = sb("til", [P, E])
        cum = sb("cum", [P, E])
        offs = sb("offs", [P, E])
        base0 = sb("base0", [P, E])
        base = sb("base", [P, E])
        past = sb("past", [P, E])
        te0 = sb("te0", [P, 1])
        te1 = sb("te1", [P, 1])
        te_i = sb("te_i", [1, P], I32)
        pos = sb("pos", [P, T])
        pos_i = sb("pos_i", [P, T], I32)
        tile_i = sb("tile_i", [P, T], I32)
        slot_i = sb("slot_i", [P, T], I32)
        slot_b = sb("slot_b", [P, T], BF16)
        tile_b = sb("tile_b", [P, T], BF16)
        at_slot = sb("at_slot", [P, LIST, 4, P], BF16)
        at_tile = sb("at_tile", [P, LIST, 4, NTILE], BF16)
        tok_at = sb("tok_at", [P, LIST, 4, 2, NTILE], BF16)
        col_i = sb("col_i", [P, NTILE], I32)
        seg_i = sb("seg_i", [P, NTILE], I32)
        row_i = sb("row_i", [P, NTILE], I32)
        listed = sb("listed", [P, NTILE])
        token = sb("token", [P, NTILE])
        empty = sb("empty", [P, NTILE])
        gidx = sb("gidx", [P, NTILE], I32)
        sidx = sb("sidx", [P, NTILE], I32)
        gcol = sb("gcol", [P, SLOTS, 2], I32)
        scol = sb("scol", [P, SLOTS, 2], I32)
        xT2 = sb("xT2", [P, C, 2, P])
        w1_now = sb("w1_now", [P, SLOTS, 2, C * HID])
        w2_now = sb("w2_now", [HID + 1, SLOTS, 2, D + 1])
        hT = sb("hT", [HID + 1, 2, P])
        yb = sb("yb", [P, SLOTS, 2, D])
        xa = sb("xa", [P, C, P])
        qT = sb("qT", [P, C, P])
        v = sb("v", [P, NH // 2, 2, VS])
        nmax = sb("nmax", [P, NH])
        psum = sb("psum", [P, NH])
        pinv = sb("pinv", [P, NH])
        rinv = sb("rinv", [P, NH, DH])
        rinvT = sb("rinvT", [P, C, P])
        oT = sb("oT", [P, C, P])
        att = sb("att", [P, NSEG, D])
        xg = xin[:, 0:SLOTS, 0:2, :]
        xn2 = xT1[:, :, :, :, :].rearrange("p u c r n -> p (u c r n)")[:, 0:SLOTS * 2 * D]\
            .rearrange("p (s t c) -> p s t c", s=SLOTS, t=2)
        kT = onehot[:, :, :].rearrange("p e t -> p (e t)").rearrange("p (c m n) -> p c m n", c=C, m=8)[:, :, 0:4, :]
        probs = count[:, :, :].rearrange("p e t -> p (e t)").rearrange("p (n k) -> p n k", k=P)
        probsT = place[:, :, :].rearrange("p e t -> p (e t)").rearrange("p (n k) -> p n k", k=P)

        bank = [ctx.enter_context(nc.psum_tensor(f"bank{i}", [P, 512], FP32)) for i in range(8)]
        b_o, b_v_k, b_x, b_y = bank[4], bank[6], bank[5], bank[7]

        x_seg = x.rearrange("b (s p r) c -> (b s) p (r c)", p=P, r=R)
        out_rows = out.rearrange("b n c -> (b n) c")
        rows = nc.dram_tensor("rows", [NTOK, ROW], FP32, kind="Internal").ap()
        rows_seg = rows.rearrange("(s p r) c -> s p (r c)", p=P, r=R)
        att_rows = out.rearrange("b (s p r) c -> p (b s) r c", p=P, r=R)[:, :, 0, :]

        passed_dve = sem("passed_dve")
        passed_pe = sem("passed_pe")
        passed_pool = sem("passed_pool")
        pool_set = sem("pool_set")
        const_in = sem("const_in")
        w_attn_in = sem("w_attn_in")
        w_rout_in = sem("w_rout_in")
        w_exp_in = sem("w_exp_in")
        bias_made = sem("bias_made")
        x_in = [sem(f"x_in{u}") for u in range(U1)]
        x_out = [sem(f"x_out{u}") for u in range(U1)]
        st1_done = sem("st1_done")
        mv1_done = sem("mv1_done")
        sd1_done = sem("sd1_done")
        rs1_done = sem("rs1_done")
        ms1_done = sem("ms1_done")
        nb1_done = sem("nb1_done")
        xn1_act = sem("xn1_act")
        xn1_dve = sem("xn1_dve")
        tr1_done = sem("tr1_done")
        xT1_done = sem("xT1_done")
        xTa_done = sem("xTa_done")
        lgT_psum = sem("lgT_psum")
        lgT_done = sem("lgT_done")
        lg_psum = sem("lg_psum")
        lg_done = sem("lg_done")
        rt_step = sem("rt_step")
        oh_done = sem("oh_done")
        dsp = sem("dsp")
        tot_ready = sem("tot_ready")
        tot_psum = sem("tot_psum")
        te_ready = sem("te_ready")
        te_psum = sem("te_psum")
        te_done = sem("te_done")
        slot_oh = sem("slot_oh")
        tile_oh = sem("tile_oh")
        part_done = sem("part_done")
        col_done = sem("col_done")
        list_mm = sem("list_mm")
        idx_done = sem("idx_done")
        gcol_set = sem("gcol_set")
        scol_set = sem("scol_set")
        gathered = [sem(f"gathered{s}") for s in range(SLOTS)]
        scattered = [sem(f"scattered{s}") for s in range(SLOTS)]
        xn2_done = sem("xn2_done")
        tr2_done = sem("tr2_done")
        xT2_done = sem("xT2_done")
        h_psum = sem("h_psum")
        w_now_in = [sem(f"w_now_in{s}") for s in range(SLOTS)]
        hT_done = sem("hT_done")
        y_psum = sem("y_psum")
        y_done = sem("y_done")
        ones_set = sem("ones_set")
        xa_in = sem("xa_in")
        v_psum = sem("v_psum")
        v_done = sem("v_done")
        q_psum = sem("q_psum")
        k_psum = sem("k_psum")
        q_done = sem("q_done")
        k_done = sem("k_done")
        s_psum = sem("s_psum")
        max_done = sem("max_done")
        exp_done = sem("exp_done")
        pt_psum = sem("pt_psum")
        pt_dve = sem("pt_dve")
        pt_act = sem("pt_act")
        o_psum = sem("o_psum")
        pinv_done = sem("pinv_done")
        rinv_done = sem("rinv_done")
        rinvT_psum = sem("rinvT_psum")
        rinvT_done = sem("rinvT_done")
        oT_done = sem("oT_done")
        r_psum = sem("r_psum")
        att_done = sem("att_done")
        added = sem("added")

        block = ctx.enter_context(nc.Block())

        @block.sync
        def _(sp):
            def load_x(k, u):
                seg = x_seg[k] if isinstance(k, int) else x_seg[bass.ds(k, 1)].rearrange("a p n -> (a p) n")
                sp.dma_start(xin[:, u, :, 0:D], seg.rearrange("p (r c) -> p r c", r=R)).then_inc(x_in[u], 16)

            load_x(0, 0)
            load_x(1, 1)
            sp.dma_start(r_w_s[:, :, :], r_w).then_inc(w_rout_in, 16)
            for r in range(R):
                sp.dma_start(r_b_s[r * E:(r + 1) * E, :], r_b.rearrange("(e a) -> e a", a=1)).then_inc(w_rout_in, 16)
            for u in range(2, U1):
                load_x(u, u)
            sp.dma_start(heads4[:, :], consts).then_inc(const_in, 16)
            sp.dma_start(b_qk_s[:, :], b_qk).then_inc(const_in, 16)
            sp.dma_start(w_in_s[:, :, :], w_in).then_inc(w_attn_in, 16)
            sp.dma_start(w_out_s[:, :, :], w_out).then_inc(w_attn_in, 16)
            sp.dma_start(b_v_s[:, :], b_v.rearrange("(a n) -> a n", a=1).broadcast_to([P, D])).then_inc(w_attn_in, 16)
            sp.dma_start(b_out_s[:, :], b_out.rearrange("(a n) -> a n", a=1).broadcast_to([P, D]))\
                .then_inc(w_attn_in, 16)

            def router_steps(i, later, more):
                for u in range(U1):
                    k = i * U1 + u
                    sp.wait_ge(rs1_done, k + 1)
                    seg = rows_seg[k] if isinstance(k, int) else rows_seg[bass.ds(k, 1)].rearrange("a p n -> (a p) n")
                    sp.dma_start(seg, xin[:, u, :, :].rearrange("p r c -> p (r c)")).then_inc(x_out[u], 16)
                    if (later or u) and (more or not u):
                        b = (u - 1) % U1
                        sp.wait_ge(x_out[b], (i + (u > 0)) * 16)
                        sp.wait_ge(xn1_act, k)
                        sp.wait_ge(xn1_dve, k)
                        load_x(k + U1 - 1, b)

            router_steps(0, False, True)
            with sp.Fori(1, NSEG // U1 - 1) as i:
                router_steps(i, True, True)
            router_steps(NSEG // U1 - 1, True, False)
            sp.dma_start(w1_s[:, :, :], w1).then_inc(w_exp_in, 16)
            sp.dma_start(w2_s[:, :, :], w2).then_inc(w_exp_in, 16)

            def segment_in(i, later):
                if later:
                    sp.wait_ge(v_psum, i)
                    sp.wait_ge(q_psum, i)
                    sp.wait_ge(k_psum, i)
                sp.dma_start(xa[:, :, :].rearrange("p c n -> p (c n)"),
                             xTa[:, bass.ds(i, 1), :, :].rearrange("p a c n -> p (a c n)")).then_inc(xa_in, 16)

            def expert_in(s, n, experts, later):
                if later:
                    sp.wait_ge(y_psum, n - SLOTS + 1)
                for t in range(2):
                    sp.dma_start(w1_now[:, s, t, :],
                                 w1_s[:, bass.ds(experts[t], 1), :].rearrange("p a n -> p (a n)"))\
                        .then_inc(w_now_in[s], 16)
                    sp.dma_start(w2_now[:, s, t, :],
                                 w2_s[:, bass.ds(experts[t], 1), :].rearrange("p a n -> p (a n)"))\
                        .then_inc(w_now_in[s], 16)

            sp.wait_ge(xTa_done, NSEG)
            segment_in(0, False)
            sp.wait_ge(te_done, 1)
            sp.wait_ge(w_exp_in, 32)

            def loop_step(i, later):
                experts = [sp.value_load(te_i[0:1, bass.ds(i * 2 * SLOTS + m, 1)], min_val=0, max_val=E - 1)
                           for m in range(2 * SLOTS)]
                if later:
                    segment_in(i, later)
                for s in range(SLOTS):
                    expert_in(s, i * SLOTS + s, experts[2 * s:2 * s + 2], later)

            loop_step(0, False)
            with sp.Fori(1, NSEG) as i:
                loop_step(i, True)

        @block.gpsimd
        def _(pool):
            done = [0]

            def step(ins):
                done[0] += 1
                ins.then_inc(pool_set, 1)

            step(pool.memset(eps[:, :], EPS))
            step(pool.memset(power[:, :], -0.5))
            step(pool.memset(zero4[:, :], 0.0))
            step(pool.memset(ident[:, :], 0.0))
            pool.wait_ge(pool_set, 4)
            step(pool.affine_select(out=ident[:, :], in_=ident[:, :], compare_op=ALU.not_equal, fill=1.0,
                                    base=0, pattern=[[-1, P]], channel_multiplier=1))
            step(pool.iota(rank_i[:, :], [[-1, E]], base=E, channel_multiplier=0))
            pool.wait_ge(pool_set, 6)
            step(pool.tensor_copy(rank[:, :], rank_i[:, :]))
            assert done[0] == SETUP_ROUTER

            def others():
                step(pool.memset(causal[:, :], 0.0))
                step(pool.memset(before[:, :], 1.0))
                step(pool.memset(onesb[:, :], 1.0))
                step(pool.memset(zeros[:, :], 0.0))
                step(pool.iota(iota_i[:, :], [[1, P]], base=0, channel_multiplier=0))
                step(pool.iota(part_i[:, :], [[0, 1]], base=0, channel_multiplier=1))
                step(pool.memset(ends[:, 0:1], 0.0))
                step(pool.memset(v[:, :, :, :], 0.0))
                pool.wait_ge(pool_set, done[0])
                step(pool.affine_select(out=causal[:, :], in_=causal[:, :], compare_op=ALU.is_ge, fill=MASK,
                                        base=0, pattern=[[-1, P]], channel_multiplier=1))
                step(pool.affine_select(out=before[:, :], in_=before[:, :], compare_op=ALU.is_gt, fill=0.0,
                                        base=0, pattern=[[1, P]], channel_multiplier=-1))
                step(pool.tensor_copy(iota[:, :], iota_i[:, :]))
                step(pool.tensor_copy(part[:, :], part_i[:, :]))
            others()
            assert done[0] == SETUP
            def keep(k, u):
                pool.wait_ge(xT1_done, k + 1)
                pool.tensor_copy(xTa[:, bass.ds(k, 1), :, :].rearrange("p a c n -> p (a c) n"),
                                 xT1[:, u % 2, :, 0, :]).then_inc(xTa_done, 1)

            def router_steps(i, later):
                for u in range(U1):
                    k = i * U1 + u
                    pool.wait_ge(mv1_done, k + 1)
                    pool.tensor_tensor(sd1[:, :], xin[:, u, :, D + 1], eps[:, :], ALU.add).then_inc(sd1_done, 1)
                    pool.wait_ge(sd1_done, k + 1)
                    pool.tensor_tensor(xin[:, u, :, D + 1], sd1[:, :], power[:, :], ALU.pow).then_inc(rs1_done, 1)
                    pool.wait_ge(rs1_done, k + 1)
                    pool.tensor_tensor(ms1[:, :], xin[:, u, :, D], xin[:, u, :, D + 1], ALU.mult).then_inc(ms1_done, 1)
                    pool.wait_ge(ms1_done, k + 1)
                    pool.tensor_tensor(nb1[:, u, :], zero4[:, :], ms1[:, :], ALU.subtract).then_inc(nb1_done, 1)
                    if later or u >= 2:
                        keep(k - 2, u)

            router_steps(0, False)
            with pool.Fori(1, NSEG // U1) as i:
                router_steps(i, True)
            keep(NSEG - 2, 0)
            keep(NSEG - 1, 1)
            def list_steps(i, later):
                for u in range(LIST):
                    n = i * LIST + u
                    pool.wait_ge(tile_oh, n + 1)
                    if later:
                        pool.wait_ge(list_mm, n - LIST + 1)
                    pool.tensor_tensor(tok_at[:, u, :, 1, :], at_tile[:, u, :, :],
                                       iota[:, bass.ds(n * 4 + 1, 4)][:, :, None].broadcast_to([P, 4, NTILE]),
                                       ALU.mult).then_inc(col_done, 1)

            list_steps(0, False)
            with pool.Fori(1, T // (4 * LIST)) as i:
                list_steps(i, True)

            def gather(s, n):
                for t in range(2):
                    pool.indirect_dma_start(out=xg[:, s, t, :], out_offset=None, in_=rows[:, :],
                                            in_offset=bass.IndirectOffsetOnAxis(ap=gcol[:, s, t:t + 1], axis=0))\
                        .then_inc(gathered[s], 16)

            pool.wait_ge(idx_done, 2)
            for s in range(SLOTS):
                pool.tensor_copy(gcol[:, s, :], gidx[:, 2 * s:2 * s + 2]).then_inc(gcol_set, 1)
            pool.wait_ge(gcol_set, SLOTS)
            for u in range(U1):
                pool.wait_ge(x_out[u], 16 * (NSEG // U1))
            for s in range(SLOTS):
                gather(s, s)

            def loop_step(i, later, last=False):
                for s in range(SLOTS):
                    n = i * SLOTS + s
                    if later:
                        pool.wait_ge(scattered[s], i * 32)
                    pool.tensor_copy(scol[:, s, :], sidx[:, bass.ds(n * 2, 2)]).then_inc(scol_set, 1)
                    pool.wait_ge(gathered[s], i * 32 + 32)
                    if not last:
                        pool.tensor_copy(gcol[:, s, :], gidx[:, bass.ds(n * 2 + 2 * SLOTS, 2)]).then_inc(gcol_set, 1)
                        pool.wait_ge(gcol_set, n + 1 + SLOTS)
                    pool.wait_ge(scol_set, n + 1)
                    pool.wait_ge(y_done, n + 1)
                    pool.sem_inc(passed_pool, 1)
                    for t in range(2):
                        pool.indirect_dma_start(out=out_rows[:, :],
                                                out_offset=bass.IndirectOffsetOnAxis(ap=scol[:, s, t:t + 1], axis=0),
                                                in_=yb[:, s, t, :], in_offset=None, bounds_check=NTOK - 1,
                                                oob_is_err=False).then_inc(scattered[s], 16)
                    if not last:
                        gather(s, n)

            loop_step(0, False)
            with pool.Fori(1, NSEG - 1) as i:
                loop_step(i, True)
            loop_step(NSEG - 1, True, True)
            for s in range(SLOTS):
                pool.wait_ge(scattered[s], 32 * NSEG)
            pool.wait_ge(att_done, NSEG - 1)
            pool.dma_start(att_rows[:, 0:NSEG - 1, :], att[:, 0:NSEG - 1, :], accum_op=ALU.add).then_inc(added, 16)
            pool.wait_ge(att_done, NSEG)
            pool.dma_start(att_rows[:, NSEG - 1:NSEG, :], att[:, NSEG - 1:NSEG, :], accum_op=ALU.add)\
                .then_inc(added, 16)
            pool.wait_ge(added, 32)

        @block.vector
        def _(dve):
            dve.memset(hT[HID:HID + 1, :, :], 1.0).then_inc(ones_set, 1)
            dve.wait_ge(pool_set, SETUP_ROUTER)

            def normalise_last(k, u):
                dve.wait_ge(rs1_done, k + 1)
                dve.tensor_scalar(xn1[:, u % 2, R - 1, :], xin[:, u, R - 1, 0:D], xin[:, u, R - 1, D:D + 1],
                                  xin[:, u, R - 1, D + 1:D + 2], ALU.subtract, ALU.mult).then_inc(xn1_dve, 1)

            n = U1 * R

            def largest(i):
                dve.wait_ge(lg_psum, i * U1)
                dve.tensor_copy(lg[:, :, :].rearrange("p r e -> p (r e)"), bank[5][:, :]).then_inc(lg_done, 1)
                dve.wait_ge(lg_done, i)
                dve.reduce_max(lmax[:, :], lg[:, :, :], AX.X).then_inc(rt_step, 1)

            def ranked(i):
                dve.wait_ge(rt_step, i * 4 - 3)
                dve.tensor_tensor(hit[:, :, :], lg[:, :, :], lmax[:, :, None].broadcast_to([P, n, E]),
                                  ALU.is_equal).then_inc(rt_step, 1)
                dve.wait_ge(rt_step, i * 4 - 2)
                dve.tensor_tensor(hit[:, :, :], hit[:, :, :], rank[:, None, :].broadcast_to([P, n, E]),
                                  ALU.mult).then_inc(rt_step, 1)

            def chosen(i):
                dve.wait_ge(rt_step, i * 4 - 1)
                dve.reduce_max(first[:, :], hit[:, :, :], AX.X).then_inc(rt_step, 1)
                dve.wait_ge(rt_step, i * 4)
                dve.tensor_tensor(onehot[:, :, bass.ds(i * n - n, n)].rearrange("p e r -> p r e"),
                                  rank[:, None, :].broadcast_to([P, n, E]),
                                  first[:, :, None].broadcast_to([P, n, E]), ALU.is_equal).then_inc(oh_done, 1)

            def router_steps(i, logits_in, logits_before):
                for u in range(U1):
                    k = i * U1 + u
                    if logits_in or u >= 2:
                        dve.wait_ge(mv1_done, k - 1)
                    dve.wait_ge(x_in[u], i * 16 + 16)
                    for r in range(R):
                        last = dve.bn_stats(st1[:, u % 2, r, :], xin[:, u, r, 0:D])
                    last.then_inc(st1_done, 1)
                    if logits_in or u:
                        if logits_in or u >= 3:
                            dve.wait_ge(tr1_done, k - 2)
                        normalise_last(k - 1, (u - 1) % U1)
                    dve.wait_ge(st1_done, k + 1)
                    dve.sem_inc(passed_dve, 1)
                    for r in range(R):
                        last = dve.bn_aggr(xin[:, u, r, D:D + 2], st1[:, u % 2, r, :])
                    last.then_inc(mv1_done, 1)
                    if logits_before and u == 0:
                        ranked(i - 1)
                    if logits_before and u == 1:
                        chosen(i - 1)
                    if logits_in and u == U1 - 1:
                        largest(i)

            router_steps(0, False, False)
            router_steps(1, True, False)
            with dve.Fori(2, NSEG // U1) as i:
                router_steps(i, True, True)
            ranked(NSEG // U1 - 1)
            dve.wait_ge(tr1_done, NSEG - 2)
            normalise_last(NSEG - 1, U1 - 1)
            chosen(NSEG // U1 - 1)
            largest(NSEG // U1)
            ranked(NSEG // U1)
            chosen(NSEG // U1)
            def values(i):
                dve.wait_ge(v_psum, i + 1)
                if not isinstance(i, int) or i:
                    dve.wait_ge(o_psum, i)
                dve.tensor_tensor(v[:, :, :, 0:DH], b_v_k[:, 0:D].rearrange("p (h e d) -> p h e d", e=2, d=DH),
                                  b_v_s[:, :].rearrange("p (h e d) -> p h e d", e=2, d=DH), ALU.add)\
                    .then_inc(v_done, 1)

            steps = [0]

            def step(ins):
                steps[0] += 1
                ins.then_inc(dsp, 1)
                dve.wait_ge(dsp, steps[0])

            dve.wait_ge(pool_set, SETUP)
            dve.wait_ge(oh_done, NSEG // U1)
            oh_flat = onehot[:, :, :].rearrange("p e t -> p (e t)")
            step(dve.tensor_tensor_scan(count[:, :, :].rearrange("p e t -> p (e t)"), oh_flat, oh_flat, 0.0,
                                        ALU.add, ALU.max))
            step(dve.tensor_copy(ends[:, 1:E + 1], count[:, :, T - 1]))
            dve.tensor_tensor(rowtot[:, :], ends[:, 1:E + 1], ends[:, 0:E], ALU.subtract).then_inc(tot_ready, 1)
            dve.wait_ge(tot_psum, 1)
            step(dve.tensor_scalar(cnt_i[:, :], bank[0][:, E:2 * E], float(P - 1), None, ALU.add))
            step(dve.tensor_scalar(til_i[:, :], cnt_i[:, :], 7, None, ALU.arith_shift_right))
            step(dve.tensor_copy(til[:, :], til_i[:, :]))
            step(dve.tensor_tensor_scan(cum[:, :], til[:, :], til[:, :], 0.0, ALU.add, ALU.max))
            step(dve.tensor_scalar(past[:, :], cum[:, :], part[:, 0:1], None, ALU.is_le))
            step(dve.reduce_sum(te0[:, :], past[:, :], AX.X))
            dve.tensor_scalar(te1[:, :], te0[:, :], float(E - 1), None, ALU.min).then_inc(te_ready, 1)
            step(dve.tensor_tensor(offs[:, :], cum[:, :], til[:, :], ALU.subtract))
            step(dve.scalar_tensor_tensor(base0[:, :], offs[:, :], float(P), bank[0][:, 0:E], ALU.mult, ALU.add))
            step(dve.scalar_tensor_tensor(base[:, :], base0[:, :], -1.0, ends[:, 0:E], ALU.add, ALU.subtract))
            step(dve.tensor_tensor(place[:, :, :], count[:, :, :], base[:, :, None].broadcast_to([P, E, T]), ALU.add))
            dve.wait_ge(w_attn_in, 64)
            values(0)
            step(dve.tensor_tensor(place[:, :, :], place[:, :, :], onehot[:, :, :], ALU.mult))
            step(dve.reduce_sum(pos[:, :], place[:, :, :].rearrange("p e t -> p t e"), AX.X))
            step(dve.tensor_copy(pos_i[:, :], pos[:, :]))
            dve.tensor_scalar(slot_i[:, :], pos_i[:, :], P - 1, None, ALU.bitwise_and)
            step(dve.tensor_scalar(tile_i[:, :], pos_i[:, :], 7, None, ALU.arith_shift_right))
            step(dve.tensor_copy(slot_b[:, :], slot_i[:, :]))
            step(dve.tensor_copy(tile_b[:, :], tile_i[:, :]))
            dve.wait_ge(te_psum, 1)
            dve.tensor_copy(te_i[0:1, :], bank[1][0:1, 0:P]).then_inc(te_done, 1)

            def list_steps(i, later):
                for u in range(LIST):
                    n = i * LIST + u
                    if later:
                        dve.wait_ge(list_mm, n - LIST + 1)
                    dve.tensor_tensor(at_tile[:, u, :, :], iota[:, None, 0:NTILE].broadcast_to([P, 4, NTILE]),
                                      tile_b[:, bass.ds(n * 4, 4)][:, :, None].broadcast_to([P, 4, NTILE]),
                                      ALU.is_equal).then_inc(tile_oh, 1)
                    dve.tensor_tensor(at_slot[:, u, :, :], iota[:, None, :].broadcast_to([P, 4, P]),
                                      slot_b[:, bass.ds(n * 4, 4)][:, :, None].broadcast_to([P, 4, P]),
                                      ALU.is_equal).then_inc(slot_oh, 1)

            list_steps(0, False)
            with dve.Fori(1, T // (4 * LIST)) as i:
                list_steps(i, True)
            dve.wait_ge(list_mm, T // 4 + 1)
            step(dve.tensor_scalar(col_i[:, :], bank[2][:, NTILE:2 * NTILE], -1.0, 0.0, ALU.add, ALU.max))
            dve.tensor_scalar(seg_i[:, :], col_i[:, :], 2, None, ALU.arith_shift_right)
            step(dve.tensor_scalar(row_i[:, :], col_i[:, :], R - 1, None, ALU.bitwise_and))
            step(dve.scalar_tensor_tensor(listed[:, :], bank[2][:, 0:NTILE], float(R), row_i[:, :], ALU.mult, ALU.add))
            dve.scalar_tensor_tensor(token[:, :], seg_i[:, :], float(P * R), listed[:, :], ALU.mult, ALU.add)
            step(dve.tensor_scalar(empty[:, :], bank[2][:, NTILE:2 * NTILE], 0.0, FAR, ALU.is_equal, ALU.mult))
            dve.tensor_copy(gidx[:, :], token[:, :]).then_inc(idx_done, 1)
            dve.tensor_tensor(sidx[:, :], token[:, :], empty[:, :], ALU.add).then_inc(idx_done, 1)

            def normalise(s, n, turn):
                dve.wait_ge(gathered[s], turn * 32 + 32)
                for t in range(2):
                    last = dve.tensor_scalar(xn2[:, s, t, :], xg[:, s, t, 0:D], xg[:, s, t, D:D + 1],
                                             xg[:, s, t, D + 1:D + 2], ALU.subtract, ALU.mult)
                last.then_inc(xn2_done, 1)

            def sums(s, n, i, later):
                dve.wait_ge(y_psum, n + 1)
                if later:
                    dve.wait_ge(scattered[s], i * 32)
                dve.scalar_tensor_tensor(yb[:, s, :, :], b_y[:, :].rearrange("p (t c) -> p t c", t=2), 0.0,
                                         xg[:, s, :, 0:D], ALU.max, ALU.add).then_inc(y_done, 1)

            def turn_probs(j, i):
                dve.wait_ge(pt_psum, i * BANKS + j + 1)
                dve.tensor_copy(probsT[:, 4 * j:4 * j + 4, :].rearrange("p n k -> p (n k)"), bank[j][:, :])\
                    .then_inc(pt_dve, 1)

            def invert(i):
                dve.wait_ge(exp_done, i * BANKS + BANKS)
                dve.reciprocal(pinv[:, :], psum[:, :]).then_inc(pinv_done, 1)
                dve.wait_ge(pinv_done, i + 1)
                dve.tensor_copy(rinv[:, :, :], pinv[:, :, None].broadcast_to([P, NH, DH])).then_inc(rinv_done, 1)

            def hidden(s, n):
                dve.wait_ge(h_psum, n + 1)
                for t in range(2):
                    last = dve.tensor_scalar(hT[0:HID, t, :], b_x[t * HID:(t + 1) * HID, 0:P],
                                             w2_now[0:HID, s, t, D:D + 1], 0.0, ALU.add, ALU.max)
                last.then_inc(hT_done, 1)

            def norm_out(i):
                dve.wait_ge(o_psum, i)
                dve.wait_ge(rinvT_done, i)
                dve.tensor_tensor(oT[:, :, :].rearrange("p c n -> p (c n)"), b_o[:, 0:D],
                                  rinvT[:, :, :].rearrange("p c n -> p (c n)"), ALU.mult).then_inc(oT_done, 1)

            def bias_out(i):
                dve.wait_ge(r_psum, i)
                dve.tensor_tensor(att[:, bass.ds(i - 1, 1), :].rearrange("p a c -> p (a c)"), b_o[:, 0:D],
                                  b_out_s[:, :], ALU.add).then_inc(att_done, 1)

            def keys(g, i):
                dve.wait_ge(k_psum, i + 1)
                dve.scalar_tensor_tensor(
                    kT[:, g, :, :], b_v_k[:, g * P:(g + 1) * P][:, None, :].broadcast_to([P, 4, P]),
                    b_qk_s[:, C + g:C + g + 1], heads4[:, :, None].broadcast_to([P, 4, P]), ALU.add, ALU.mult)\
                    .then_inc(k_done, 1)

            def maxima(j, i):
                dve.wait_ge(s_psum, i * BANKS + j + 1)
                if not isinstance(i, int) or i:
                    dve.wait_ge(pt_psum, i * BANKS)
                dve.sem_inc(passed_dve, 1)
                for m in range(4):
                    h = 4 * j + m
                    last = dve.tensor_tensor_reduce(probs[:, h, :], bank[j][:, m * P:(m + 1) * P], causal[:, :],
                                                    1.0, HIGH, ALU.add, ALU.min, nmax[:, h:h + 1])
                last.then_inc(max_done, 1)

            dve.wait_ge(const_in, 32)
            for g in range(C):
                keys(g, 0)
            maxima(0, 0)
            maxima(1, 0)
            normalise(0, 0, 0)
            maxima(2, 0)
            normalise(1, 1, 0)
            maxima(3, 0)
            normalise(2, 2, 0)
            turn_probs(0, 0)
            sums(0, 0, 0, False)
            turn_probs(1, 0)
            keys(0, 1)
            keys(1, 1)
            turn_probs(2, 0)
            sums(1, 1, 0, False)
            hidden(2, 2)
            sums(2, 2, 0, False)
            normalise(0, SLOTS, 1)

            def loop_step(i, last=False):
                n = i * SLOTS
                normalise(1, n + 1, i)
                invert(i - 1)
                norm_out(i)
                values(i)
                sums(0, n, i, True)
                bias_out(i)
                normalise(2, n + 2, i)
                maxima(0, i)
                sums(1, n + 1, i, True)
                if last:
                    hidden(2, n + 2)
                maxima(1, i)
                if last:
                    sums(2, n + 2, i, True)
                maxima(2, i)
                maxima(3, i)
                if not last:
                    hidden(2, n + 2)
                    normalise(0, n + 3, i + 1)
                turn_probs(0, i)
                if not last:
                    keys(0, i + 1)
                    keys(1, i + 1)
                    turn_probs(1, i)
                    sums(2, n + 2, i, True)
                else:
                    turn_probs(1, i)
                turn_probs(2, i)

            with dve.Fori(1, NSEG - 1) as i:
                loop_step(i)
            loop_step(NSEG - 1, True)
            invert(NSEG - 1)
            norm_out(NSEG)
            bias_out(NSEG)

        @block.scalar
        def _(act):
            def turn_x1(k, u):
                act.wait_ge(tr1_done, k + 1)
                if not isinstance(k, int) or k >= 2:
                    act.wait_ge(xTa_done, k - 1)
                for c in range(C):
                    last = act.activation(xT1[:, u % 2, c, :, :].rearrange("p r n -> p (r n)"),
                                          bank[2 * (u % 2) + c][:, :], ACT.Copy)
                last.then_inc(xT1_done, 1)

            def logits_out(k, u):
                act.wait_ge(lgT_psum, k + 1)
                act.activation(lgT[:, u % 2, :], bank[4 + 2 * (u % 2)][:, 0:P], ACT.Identity, bias=r_b_s[:, 0:1])\
                    .then_inc(lgT_done, 1)

            act.wait_ge(pool_set, 1)
            act.activation(warm[:, :], eps[:, :], ACT.Identity)
            act.wait_ge(w_rout_in, 16 + 16 * R)

            def router_steps(i, later):
                for u in range(U1):
                    k = i * U1 + u
                    act.wait_ge(nb1_done, k + 1)
                    if later or u >= 2:
                        act.wait_ge(tr1_done, k - 1)
                    for r in range(R - 1):
                        last = act.activation(xn1[:, u % 2, r, :], xin[:, u, r, 0:D], ACT.Identity,
                                              scale=xin[:, u, r, D + 1:D + 2], bias=nb1[:, u, r:r + 1])
                    last.then_inc(xn1_act, 1)
                    if later or u:
                        turn_x1(k - 1, (u - 1) % U1)
                    if later or u >= 2:
                        logits_out(k - 2, (u - 2) % U1)

            router_steps(0, False)
            with act.Fori(1, NSEG // U1) as i:
                router_steps(i, True)
            turn_x1(NSEG - 1, U1 - 1)
            logits_out(NSEG - 2, U1 - 2)
            logits_out(NSEG - 1, U1 - 1)
            act.wait_ge(const_in, 32)
            act.activation(q_bias[:, :], b_qk_s[:, 0:C], ACT.Copy, scale=-DH ** -0.5).then_inc(bias_made, 1)

            def turn_probs(i):
                j = BANKS - 1
                act.wait_ge(pt_psum, i * BANKS + BANKS)
                act.activation(probsT[:, 4 * j:4 * j + 4, :].rearrange("p n k -> p (n k)"), bank[j][:, :], ACT.Copy)\
                    .then_inc(pt_act, 1)

            def turn_x(n):
                act.wait_ge(tr2_done, n + 1)
                act.activation(xT2[:, :, :, :].rearrange("p c t n -> p (c t n)"), b_x[:, :], ACT.Copy)\
                    .then_inc(xT2_done, 1)

            def hidden(s, n):
                act.wait_ge(h_psum, n + 1)
                for t in range(2):
                    last = act.activation(hT[0:HID, t, :], b_x[t * HID:(t + 1) * HID, 0:P], ACT.Relu,
                                          bias=w2_now[0:HID, s, t, D:D + 1])
                last.then_inc(hT_done, 1)

            def queries(i):
                act.wait_ge(q_psum, i + 1)
                for c in range(C):
                    last = act.activation(qT[:, c, :], b_o[:, c * P:(c + 1) * P], ACT.Identity, scale=-DH ** -0.5,
                                          bias=q_bias[:, c:c + 1])
                last.then_inc(q_done, 1)

            def turn_sums(i):
                act.wait_ge(rinvT_psum, i)
                act.activation(rinvT[:, :, :].rearrange("p c n -> p (c n)"), b_o[:, D:2 * D], ACT.Copy)\
                    .then_inc(rinvT_done, 1)

            def exps(j, i):
                act.wait_ge(max_done, i * BANKS + j + 1)
                for m in range(4):
                    last = act.activation(probs[:, 4 * j + m, :], probs[:, 4 * j + m, :], ACT.Exp, scale=-1.0,
                                          bias=nmax[:, 4 * j + m:4 * j + m + 1],
                                          accum_out=psum[:, 4 * j + m:4 * j + m + 1])
                last.then_inc(exp_done, 1)

            act.wait_ge(bias_made, 1)
            queries(0)

            def list_steps(i, later):
                for u in range(LIST):
                    n = i * LIST + u
                    act.wait_ge(tile_oh, n + 1)
                    if later:
                        act.wait_ge(list_mm, n - LIST + 1)
                    act.activation(tok_at[:, u, :, 0, :], at_tile[:, u, :, :], ACT.Identity, scale=part[:, 0:1])\
                        .then_inc(part_done, 1)

            act.wait_ge(pool_set, SETUP)
            list_steps(0, False)
            with act.Fori(1, T // (4 * LIST)) as i:
                list_steps(i, True)

            exps(0, 0)
            exps(1, 0)
            turn_x(0)
            exps(2, 0)
            hidden(0, 0)
            exps(3, 0)
            turn_x(1)
            hidden(1, 1)
            turn_x(2)

            def loop_step(i, last=False):
                n = i * SLOTS
                turn_x(n)
                turn_probs(i - 1)
                hidden(0, n)
                turn_sums(i)
                turn_x(n + 1)
                hidden(1, n + 1)
                queries(i)
                turn_x(n + 2)
                exps(0, i)
                exps(1, i)
                exps(2, i)
                exps(3, i)

            with act.Fori(1, NSEG - 1) as i:
                loop_step(i)
            loop_step(NSEG - 1, True)
            turn_probs(NSEG - 1)
            turn_sums(NSEG)

        @block.tensor
        def _(pe):
            pe.wait_ge(pool_set, SETUP_ROUTER)
            pe.wait_ge(w_rout_in, 16 + 16 * R)

            def transposed(k, u):
                pe.wait_ge(xn1_act, k + 1)
                pe.wait_ge(xn1_dve, k + 1)
                for c in range(C):
                    for r in range(R):
                        last = pe.transpose(bank[2 * (u % 2) + c][:, r * P:(r + 1) * P],
                                            xn1[:, u % 2, r, c * P:(c + 1) * P], ident[:, :])
                last.then_inc(tr1_done, 1)

            def logits(k, u, after):
                pe.wait_ge(xT1_done, k + 1)
                if after:
                    pe.wait_ge(lgT_done, k - 1)
                for c in range(C):
                    for r in range(R):
                        last = pe.matmul(bank[4 + 2 * (u % 2)][r * E:(r + 1) * E, 0:P], r_w_s[:, c, :],
                                         xT1[:, u % 2, c, r, :], start=(c == 0), stop=(c == C - 1))
                last.then_inc(lgT_psum, 1)

            def logits_back(k, u, i, copied):
                pe.wait_ge(lgT_done, k + 1)
                if copied:
                    pe.wait_ge(lg_done, i)
                pe.sem_inc(passed_pe, 1)
                pe.transpose(bank[5][:, u * P:(u + 1) * P], lgT[:, u % 2, :], ident[:, :]).then_inc(lg_psum, 1)

            def router_steps(i, later):
                for u in range(U1):
                    k = i * U1 + u
                    transposed(k, u)
                    if later or u:
                        logits(k - 1, (u - 1) % U1, later or u >= 3)
                    if later or u >= 2:
                        logits_back(k - 2, (u - 2) % U1, i, later and u == 2)

            router_steps(0, False)
            with pe.Fori(1, NSEG // U1) as i:
                router_steps(i, True)
            logits(NSEG - 1, U1 - 1, True)
            logits_back(NSEG - 2, U1 - 2, 0, False)
            logits_back(NSEG - 1, U1 - 1, 0, False)
            pe.wait_ge(tot_ready, 1)
            pe.wait_ge(pool_set, SETUP)
            pe.matmul(bank[0][:, 0:E], before[:, :], rowtot[:, :], start=True, stop=True)
            pe.matmul(bank[0][:, E:2 * E], onesb[:, :], rowtot[:, :], start=True, stop=True).then_inc(tot_psum, 1)
            pe.wait_ge(te_ready, 1)
            pe.matmul(bank[1][0:1, 0:P], te1[:, 0:1], ident[:, :], start=True, stop=True).then_inc(te_psum, 1)
            def turn_x(s, n, later):
                pe.wait_ge(xn2_done, n + 1)
                if later:
                    pe.wait_ge(hT_done, n)
                for c in range(C):
                    for t in range(2):
                        last = pe.transpose(b_x[:, (2 * c + t) * P:(2 * c + t + 1) * P],
                                            xn2[:, s, t, c * P:(c + 1) * P], ident[:, :])
                last.then_inc(tr2_done, 1)

            def hidden(s, n, i):
                pe.wait_ge(xT2_done, n + 1)
                pe.wait_ge(w_now_in[s], i * 64 + 64)
                for c in range(C):
                    for t in range(2):
                        last = pe.matmul(b_x[t * HID:(t + 1) * HID, 0:P], w1_now[:, s, t, c * HID:(c + 1) * HID],
                                         xT2[:, c, t, :], start=(c == 0), stop=(c == C - 1))
                last.then_inc(h_psum, 1)

            def outputs(s, n, later):
                pe.wait_ge(hT_done, n + 1)
                if later:
                    pe.wait_ge(y_done, n)
                for t in range(2):
                    last = pe.matmul(b_y[:, t * D:(t + 1) * D], hT[:, t, :], w2_now[:, s, t, 0:D],
                                     start=True, stop=True)
                last.then_inc(y_psum, 1)

            def turn_sums(i):
                pe.wait_ge(rinv_done, i)
                flat = rinv[:, :, :].rearrange("p h d -> p (h d)")
                for c in range(C):
                    last = pe.transpose(b_o[:, D + c * P:D + (c + 1) * P], flat[:, c * P:(c + 1) * P], ident[:, :])
                last.then_inc(rinvT_psum, 1)

            def attend(i):
                pe.wait_ge(pt_dve, i * (BANKS - 1))
                pe.wait_ge(pt_act, i)
                pe.wait_ge(v_done, i)
                pe.wait_ge(q_done, i)
                for h in range(NH):
                    pair = h // 2
                    rows_h = slice(2 * DH * (pair % 4), 2 * DH * (pair % 4 + 1))
                    v_pair = v[:, pair, :, :].rearrange("p e m -> p (e m)")
                    last = pe.matmul(b_o[rows_h, pair // 4 * P:(pair // 4 + 1) * P],
                                     v_pair[:, h % 2 * 2 * DH:(h % 2 + 1) * 2 * DH],
                                     probsT[:, h, :], start=(h % 2 == 0), stop=(h % 2 == 1))
                last.then_inc(o_psum, 1)

            def project(i):
                pe.wait_ge(oT_done, i)
                for c in range(C):
                    last = pe.matmul(b_o[:, 0:D], oT[:, c, :], w_out_s[:, c, :], start=(c == 0), stop=(c == C - 1))
                last.then_inc(r_psum, 1)

            def values(i, later):
                if later:
                    pe.wait_ge(k_done, i * C + C)
                for c in range(C):
                    last = pe.matmul(b_v_k[:, 0:D], xa[:, c, :], w_in_s[:, c, 2 * D:3 * D], start=(c == 0),
                                     stop=(c == C - 1))
                last.then_inc(v_psum, 1)

            def projected(to, first, count_up):
                for g in range(C):
                    for c in range(C):
                        last = pe.matmul(to[:, g * P:(g + 1) * P], w_in_s[:, c, first + g * P:first + (g + 1) * P],
                                         xa[:, c, :], start=(c == 0), stop=(c == C - 1))
                last.then_inc(count_up, 1)

            def keys(i, values_before):
                pe.wait_ge(xa_in, i * 16 + 16)
                pe.wait_ge(v_done, values_before)
                projected(b_v_k, D, k_psum)

            def queries(i, later):
                if later:
                    pe.wait_ge(att_done, i)
                projected(b_o, 0, q_psum)

            def scores(j, i):
                pe.wait_ge(q_done, i + 1)
                pe.wait_ge(k_done, i * C + 1 + j // 2)
                if not isinstance(i, int) or i:
                    pe.wait_ge(pt_dve, i * (BANKS - 1))
                    pe.wait_ge(pt_act, i)
                half = slice(j % 2 * P // 2, (j % 2 + 1) * P // 2)
                pe.matmul(bank[j][:, :], qT[half, j // 2, :], kT[half, j // 2, :, :].rearrange("p m n -> p (m n)"),
                          start=True, stop=True).then_inc(s_psum, 1)

            def turn_probs(j, i):
                pe.wait_ge(exp_done, i * BANKS + j + 1)
                for m in range(4):
                    last = pe.transpose(bank[j][:, m * P:(m + 1) * P], probs[:, 4 * j + m, :], ident[:, :])
                last.then_inc(pt_psum, 1)

            pe.wait_ge(w_attn_in, 64)
            pe.wait_ge(xa_in, 16)
            values(0, False)
            keys(0, 1)
            queries(0, False)
            pe.matmul(bank[2][:, 0:2 * NTILE], onesb[:, :], zeros[:, :], start=True, stop=False)

            def list_steps(i, later):
                for u in range(LIST):
                    n = i * LIST + u
                    pe.wait_ge(slot_oh, n + 1)
                    pe.wait_ge(part_done, n + 1)
                    pe.wait_ge(col_done, n + 1)
                    for m in range(4):
                        last = pe.matmul(bank[2][:, 0:2 * NTILE], at_slot[:, u, m, :],
                                         tok_at[:, u, m, :, :].rearrange("p a n -> p (a n)"),
                                         start=False, stop=False)
                    last.then_inc(list_mm, 1)

            list_steps(0, False)
            with pe.Fori(1, T // (4 * LIST)) as i:
                list_steps(i, True)
            pe.matmul(bank[2][:, 0:2 * NTILE], onesb[:, :], zeros[:, :], start=False, stop=True).then_inc(list_mm, 1)

            pe.wait_ge(idx_done, 2)
            pe.wait_ge(ones_set, 1)
            scores(0, 0)
            scores(1, 0)
            scores(2, 0)
            turn_x(0, 0, False)
            scores(3, 0)
            hidden(0, 0, 0)
            turn_probs(0, 0)
            turn_x(1, 1, True)
            outputs(0, 0, False)
            turn_probs(1, 0)
            hidden(1, 1, 0)
            keys(1, 1)
            turn_probs(2, 0)
            outputs(1, 1, True)
            turn_x(2, 2, True)
            hidden(2, 2, 0)
            outputs(2, 2, True)

            def loop_step(i, last=False):
                n = i * SLOTS
                turn_x(0, n, True)
                turn_probs(3, i - 1)
                values(i, True)
                hidden(0, n, i)
                attend(i)
                turn_sums(i)
                turn_x(1, n + 1, True)
                outputs(0, n, True)
                project(i)
                hidden(1, n + 1, i)
                queries(i, True)
                outputs(1, n + 1, True)
                scores(0, i)
                turn_x(2, n + 2, True)
                if last:
                    hidden(2, n + 2, i)
                scores(1, i)
                if last:
                    outputs(2, n + 2, True)
                scores(2, i)
                scores(3, i)
                turn_probs(0, i)
                if not last:
                    hidden(2, n + 2, i)
                turn_probs(1, i)
                if not last:
                    keys(i + 1, i + 1)
                    outputs(2, n + 2, True)
                turn_probs(2, i)

            with pe.Fori(1, NSEG - 1) as i:
                loop_step(i)
            loop_step(NSEG - 1, True)
            turn_probs(3, NSEG - 1)
            attend(NSEG)
            turn_sums(NSEG)
            project(NSEG)


def kernel(L0_attn_x, L0_attn_w_in, L0_attn_b_in, L0_attn_w_out, L0_attn_b_out, L0_ffn_router_w, L0_ffn_router_b,
           L0_ffn_weights1, L0_ffn_bias1, L0_ffn_weights2, L0_ffn_bias2):
    import concourse.bacc as bacc
    import numpy as np
    from concourse.bass_utils import run_bass_kernel_spmd

    def rows(a):
        a = np.asarray(a)
        return np.ascontiguousarray(a.reshape(C, P, a.shape[1]).transpose(1, 0, 2))

    b_in = np.asarray(L0_attn_b_in)
    w1 = np.asarray(L0_ffn_weights1).reshape(E, C, P, HID).transpose(2, 0, 1, 3)
    w2 = np.zeros((HID + 1, E, D + 1), np.float32)
    w2[:HID, :, :D] = np.asarray(L0_ffn_weights2).transpose(1, 0, 2)
    w2[HID, :, :D] = np.asarray(L0_ffn_bias2)
    w2[:HID, :, D] = np.asarray(L0_ffn_bias1).T
    consts = np.arange(P)[:, None] // DH % 4 == np.arange(4)[None, :]
    arrays = {
        "x": np.asarray(L0_attn_x),
        "consts": consts.astype(np.float32),
        "w_in": rows(np.asarray(L0_attn_w_in).T),
        "b_qk": np.ascontiguousarray(b_in[:2 * D].reshape(2 * C, P).T),
        "b_v": np.ascontiguousarray(b_in[2 * D:]),
        "w_out": rows(np.asarray(L0_attn_w_out).T),
        "b_out": np.asarray(L0_attn_b_out),
        "r_w": rows(np.asarray(L0_ffn_router_w).T),
        "r_b": np.asarray(L0_ffn_router_b),
        "w1": np.ascontiguousarray(w1).reshape(P, E, C * HID),
        "w2": w2,
    }
    nc = bacc.Bacc("TRN2", target_bir_lowering=False, num_devices=1)
    args = [nc.dram_tensor(f"in_{name}", a.shape, mybir.dt.from_np(a.dtype), kind="ExternalInput").ap()
            for name, a in arrays.items()]
    out = nc.dram_tensor("out", arrays["x"].shape, FP32, kind="ExternalOutput").ap()
    build(nc, *args, out)
    r = run_bass_kernel_spmd(nc, [{f"in_{name}": a for name, a in arrays.items()}], core_ids=[0])
    return r.results[0]["out"]
```
